# Optimizing a Trainium2 kernel written in Bass

```python
import numpy as np
import jax
import jax.numpy as jnp

def _softmax(x, axis=-1):
    return jax.nn.softmax(x, axis=axis)

def _gelu(x):
    return jax.nn.gelu(x, approximate=True)

def _silu(x):
    return jax.nn.silu(x)

def _sigmoid(x):
    return jax.nn.sigmoid(x)

def _layernorm(x, axis=-1, eps=1e-05):
    m = jnp.mean(x, axis=axis, keepdims=True)
    v = jnp.var(x, axis=axis, keepdims=True)
    return (x - m) / jnp.sqrt(v + eps)

def _scatter_add(tgt, idx, src, axis=0):
    return tgt.at[idx].add(src)

def _segment_sum(src, seg, n):
    return jax.ops.segment_sum(src, seg, n)
kernel_name = 'mk_decoder_preln_d1_seqx_r4_1a9427'

def setup_inputs(seed: int=0):
    np.random.seed(seed)
    _w = jnp.asarray

    def _rec_inputs():
        import jax
        import jax.numpy as jnp
        _rk = jax.random.key(seed)
        x = -0.0002928 + 1 * jax.random.normal(jax.random.fold_in(_rk, 1), (8, 112, 256), jnp.float32)
        _lenS = 112 - jax.random.randint(jax.random.fold_in(_rk, 7), (8,), 0, max(1, 112 // 4) + 1, jnp.int32)
        _lenS2 = 375 - jax.random.randint(jax.random.fold_in(_rk, 8), (8,), 0, max(1, 375 // 4) + 1, jnp.int32)
        _ctx_1024P = jax.random.normal(jax.random.fold_in(_rk, 11), (8, 16, 256), jnp.float32)
        _ctx_1024c = jax.random.dirichlet(jax.random.fold_in(_rk, 511), 0.3 * jnp.ones((16,), jnp.float32), (8, 375))
        _ctx_1024t = jnp.einsum('bsk,bkd->bsd', _ctx_1024c, _ctx_1024P)
        _ctx_1024t = _ctx_1024t * jax.lax.rsqrt(jnp.mean(jnp.square(_ctx_1024t)) + 1e-12) * 0.953939
        ctx_1024 = -1.39393e-06 + 0.999914 * (_ctx_1024t + 0.3 * jax.random.normal(jax.random.fold_in(_rk, 611), (8, 375, 256), jnp.float32))
        _validS = jnp.arange(112)[None, :] < _lenS[:, None]
        _validS2 = jnp.arange(375)[None, :] < _lenS2[:, None]
        _causal = jnp.tril(jnp.ones((112, 112), dtype=bool))
        mask_Bx1xSxS2_ik1 = jnp.where(jnp.broadcast_to(_validS2[:, None, None, :], (8, 1, 112, 375)), 1, 0).astype(jnp.int32)
        return (x, ctx_1024, mask_Bx1xSxS2_ik1)
    x, ctx_1024, mask_Bx1xSxS2_ik1 = _rec_inputs()

    def _L0_attn_setup():
        import jax, jax.numpy as jnp
        import numpy as np
        D_MODEL = 256
        N_HEADS = 16
        D_HEAD = D_MODEL // N_HEADS
        SEQ = 512
        BATCH = 2
        key = jax.random.key(seed)
        ks = jax.random.split(key, 9)
        s = 1.0 / np.sqrt(D_MODEL)
        inp = {'x': jax.random.normal(ks[0], (BATCH, SEQ, D_MODEL), dtype=jnp.float32), 'Wq': jax.random.uniform(ks[1], (D_MODEL, D_MODEL), jnp.float32, -s, s), 'bq': jax.random.uniform(ks[2], (D_MODEL,), jnp.float32, -s, s), 'Wk': jax.random.uniform(ks[3], (D_MODEL, D_MODEL), jnp.float32, -s, s), 'bk': jax.random.uniform(ks[4], (D_MODEL,), jnp.float32, -s, s), 'Wv': jax.random.uniform(ks[5], (D_MODEL, D_MODEL), jnp.float32, -s, s), 'bv': jax.random.uniform(ks[6], (D_MODEL,), jnp.float32, -s, s), 'Wo': jax.random.uniform(ks[7], (D_MODEL, D_MODEL), jnp.float32, -s, s), 'bo': jax.random.uniform(ks[8], (D_MODEL,), jnp.float32, -s, s)}
        return inp
    _L0_attn_all = _L0_attn_setup()
    _L0_attn_in = {k: v for k, v in _L0_attn_all.items() if k in ('Wq', 'bq', 'Wk', 'bk', 'Wv', 'bv', 'Wo', 'bo')}
    del _L0_attn_all

    def _L0_xattn_setup():
        import jax, jax.numpy as jnp
        import numpy as np
        EMBED = 256
        HEADS = 16
        HEAD_DIM = EMBED // HEADS
        key = jax.random.key(seed)
        ks = jax.random.split(key, 10)
        N, S = (2, 512)
        query = jax.random.normal(ks[0], (N, S, EMBED), dtype=jnp.float32)
        key_t = jax.random.normal(ks[1], (N, S, EMBED), dtype=jnp.float32)
        value = jax.random.normal(ks[2], (N, S, EMBED), dtype=jnp.float32)
        mask = jax.random.randint(ks[3], (N, 1, S, S), 0, 2, dtype=jnp.int32)
        s = 1.0 / np.sqrt(HEAD_DIM)
        Wq = jax.random.normal(ks[4], (HEAD_DIM, HEAD_DIM), dtype=jnp.float32) * s
        Wk = jax.random.normal(ks[5], (HEAD_DIM, HEAD_DIM), dtype=jnp.float32) * s
        Wv = jax.random.normal(ks[6], (HEAD_DIM, HEAD_DIM), dtype=jnp.float32) * s
        Wo = jax.random.normal(ks[7], (EMBED, EMBED), dtype=jnp.float32) * (1.0 / np.sqrt(EMBED))
        bo = jnp.zeros((EMBED,), dtype=jnp.float32)
        return {'query': query, 'key': key_t, 'value': value, 'mask': mask, 'Wq': Wq, 'Wk': Wk, 'Wv': Wv, 'Wo': Wo, 'bo': bo}
    _L0_xattn_all = _L0_xattn_setup()
    _L0_xattn_in = {k: v for k, v in _L0_xattn_all.items() if k in ('Wq', 'Wk', 'Wv', 'Wo', 'bo')}
    del _L0_xattn_all

    def _L0_ffn_setup():
        import jax, jax.numpy as jnp
        import numpy as np
        B, S = (2, 256)
        E, TOPK = (8, 2)
        HIDDEN, HEADS, NSLOTS = (256, 4, 64)
        HEAD_K = HIDDEN // HEADS
        HEAD_V = HIDDEN // HEADS
        GATE_NORM = 8.0
        SCALE = 1.0
        EPS = 1e-05
        CHUNK = 64
        CAP = S

        def rms_norm(x, w, eps=EPS):
            y = x * jax.lax.rsqrt(jnp.mean(x * x, axis=-1, keepdims=True) + eps)
            return y * w

        def swish(x):
            return x * jax.nn.sigmoid(x)

        def gsa_chunk(q, k, v, s, g):
            EBH = q.shape[:3]
            T, Dk, Dv, M = (q.shape[3], q.shape[-1], v.shape[-1], s.shape[-1])
            Nc = T // CHUNK

            def to_chunks(x):
                return jnp.moveaxis(x.reshape(EBH + (Nc, CHUNK, x.shape[-1])), 3, 0)
            qc, kc, vc, sc, gc = map(to_chunks, (q, k, v, s, g))
            Gc = jnp.cumsum(gc, axis=-2)
            tril = jnp.tril(jnp.ones((CHUNK, CHUNK), q.dtype))
            hk0 = jnp.zeros(EBH + (Dk, M), q.dtype)
            hv0 = jnp.zeros(EBH + (M, Dv), q.dtype)

            def step(carry, xs):
                hk, hv = carry
                qt, kt, vt, st, Gt = xs
                dec = jnp.exp(Gt)
                s_in = st * jnp.exp(-Gt)
                A = jnp.einsum('ebhik,ebhjk->ebhij', qt, kt) * SCALE * tril
                ok = dec * (jnp.einsum('ebhij,ebhjm->ebhim', A, s_in) + SCALE * jnp.einsum('ebhik,ebhkm->ebhim', qt, hk))
                qv = jax.nn.softmax(ok, axis=-1)
                qvg = qv * dec
                Tm = jnp.einsum('ebhim,ebhjm->ebhij', qvg, s_in) * tril
                ov = jnp.einsum('ebhij,ebhjd->ebhid', Tm, vt) + jnp.einsum('ebhim,ebhmd->ebhid', qvg, hv)
                gl = jnp.exp(Gt[..., -1, :])
                s_rem = st * jnp.exp(Gt[..., -1:, :] - Gt)
                hk = hk * gl[..., None, :] + jnp.einsum('ebhck,ebhcm->ebhkm', kt, s_rem)
                hv = hv * gl[..., :, None] + jnp.einsum('ebhcm,ebhcd->ebhmd', s_rem, vt)
                return ((hk, hv), ov)
            _, ov = jax.lax.scan(step, (hk0, hv0), (qc, kc, vc, sc, Gc))
            return jnp.moveaxis(ov, 0, 3).reshape(EBH + (T, Dv))

        def forward(hidden_states, norm_w, Wg, Wq, Wk, Wv, Wf, gnorm_w, Wo):
            b, s, d = hidden_states.shape
            x = rms_norm(hidden_states, norm_w)
            scores = jax.nn.softmax(jnp.einsum('bsd,ed->bse', x, Wg), axis=-1)
            rw, sel = jax.lax.top_k(scores, TOPK)
            rw = rw / jnp.sum(rw, axis=-1, keepdims=True)
            routing_mask = jax.nn.one_hot(sel, E, dtype=jnp.int32).sum(2)
            s_eff = s * TOPK
            xr = jnp.repeat(x, TOPK, axis=1).reshape(b * s_eff, d)
            batch_idx = jnp.repeat(jnp.arange(b), s_eff)
            combined = batch_idx * E + sel.reshape(-1)
            sorted_indices = jnp.argsort(combined)
            x_sorted = xr[sorted_indices]
            counts = routing_mask.sum(1)
            flat_end = (jnp.cumsum(counts, axis=1) + jnp.arange(b)[:, None] * s_eff).reshape(-1)
            start = jnp.concatenate([jnp.zeros((1,), flat_end.dtype), flat_end[:-1]])
            pos = jnp.arange(CAP)[None, :] + start[:, None]
            trunc = pos + counts.reshape(-1)[:, None] - CAP
            mask = (trunc < flat_end[:, None]) & (trunc >= 0) & (trunc >= start[:, None])
            trunc = jnp.where(mask, trunc, 0)
            xe = x_sorted[trunc.reshape(-1)].reshape(b * E, CAP, d) * mask[..., None]
            xe = xe.reshape(b, E, CAP, d).transpose(1, 0, 2, 3)
            q = jnp.einsum('ebtd,kd->ebtk', xe, Wq).reshape(E, b, CAP, HEADS, HEAD_K)
            k = jnp.einsum('ebtd,ekd->ebtk', xe, Wk).reshape(E, b, CAP, HEADS, HEAD_K)
            v = jnp.einsum('ebtd,ekd->ebtk', xe, Wv).reshape(E, b, CAP, HEADS, HEAD_V)
            f = jnp.einsum('ebtd,ekd->ebtk', xe, Wf).reshape(E, b, CAP, HEADS, NSLOTS)
            g = jax.nn.log_sigmoid(f) / GATE_NORM
            slot = 1.0 - jnp.exp(g)
            q, k = (swish(q), swish(k))
            tr = lambda a: a.transpose(0, 1, 3, 2, 4)
            o = gsa_chunk(tr(q), tr(k), tr(v), tr(slot), tr(g)).transpose(0, 1, 3, 2, 4)
            gathered = o.transpose(1, 0, 2, 3, 4).reshape(b * E * CAP, HEADS, HEAD_V)
            gathered = gathered * mask.reshape(-1)[:, None, None]
            resort = jnp.zeros((b * s_eff, HEADS, HEAD_V), gathered.dtype).at[trunc.reshape(-1)].add(gathered)
            restored = resort[jnp.argsort(sorted_indices)].reshape(b, s, TOPK, HEADS, HEAD_V)
            out = (restored * rw[..., None, None]).sum(2).reshape(b, s, HIDDEN)
            return jnp.einsum('bsd,od->bso', rms_norm(out, gnorm_w), Wo)
        key = jax.random.key(seed)
        ks = jax.random.split(key, 8)
        w = 0.02
        return {'hidden_states': jax.random.normal(ks[0], (B, S, HIDDEN), jnp.float32), 'norm_w': jnp.ones((HIDDEN,), jnp.float32), 'Wg': jax.random.normal(ks[1], (E, HIDDEN), jnp.float32) * w, 'Wq': jax.random.normal(ks[2], (HIDDEN, HIDDEN), jnp.float32) * w, 'Wk': jax.random.normal(ks[3], (E, HIDDEN, HIDDEN), jnp.float32) * w, 'Wv': jax.random.normal(ks[4], (E, HIDDEN, HIDDEN), jnp.float32) * w, 'Wf': jax.random.normal(ks[5], (E, HEADS * NSLOTS, HIDDEN), jnp.float32) * w, 'gnorm_w': jnp.ones((HIDDEN,), jnp.float32), 'Wo': jax.random.normal(ks[6], (HIDDEN, HIDDEN), jnp.float32) * w}
    _L0_ffn_all = _L0_ffn_setup()
    _L0_ffn_in = {k: v for k, v in _L0_ffn_all.items() if k in ('norm_w', 'Wg', 'Wq', 'Wk', 'Wv', 'Wf', 'gnorm_w', 'Wo')}
    del _L0_ffn_all
    return {'x': x, 'ctx_1024': ctx_1024, 'mask_Bx1xSxS2_ik1': mask_Bx1xSxS2_ik1, 'L0_attn_Wq': _L0_attn_in['Wq'], 'L0_attn_bq': _L0_attn_in['bq'], 'L0_attn_Wk': _L0_attn_in['Wk'], 'L0_attn_bk': _L0_attn_in['bk'], 'L0_attn_Wv': _L0_attn_in['Wv'], 'L0_attn_bv': _L0_attn_in['bv'], 'L0_attn_Wo': _L0_attn_in['Wo'], 'L0_attn_bo': _L0_attn_in['bo'], 'L0_xattn_Wq': _L0_xattn_in['Wq'], 'L0_xattn_Wk': _L0_xattn_in['Wk'], 'L0_xattn_Wv': _L0_xattn_in['Wv'], 'L0_xattn_Wo': _L0_xattn_in['Wo'], 'L0_xattn_bo': _L0_xattn_in['bo'], 'L0_ffn_norm_w': _L0_ffn_in['norm_w'], 'L0_ffn_Wg': _L0_ffn_in['Wg'], 'L0_ffn_Wq': _L0_ffn_in['Wq'], 'L0_ffn_Wk': _L0_ffn_in['Wk'], 'L0_ffn_Wv': _L0_ffn_in['Wv'], 'L0_ffn_Wf': _L0_ffn_in['Wf'], 'L0_ffn_gnorm_w': _L0_ffn_in['gnorm_w'], 'L0_ffn_Wo': _L0_ffn_in['Wo']}

def reference(x, ctx_1024, mask_Bx1xSxS2_ik1, L0_attn_Wq, L0_attn_bq, L0_attn_Wk, L0_attn_bk, L0_attn_Wv, L0_attn_bv, L0_attn_Wo, L0_attn_bo, L0_xattn_Wq, L0_xattn_Wk, L0_xattn_Wv, L0_xattn_Wo, L0_xattn_bo, L0_ffn_norm_w, L0_ffn_Wg, L0_ffn_Wq, L0_ffn_Wk, L0_ffn_Wv, L0_ffn_Wf, L0_ffn_gnorm_w, L0_ffn_Wo):
    import jax
    import jax.numpy as jnp

    def _L0_attn_ref(x, Wq, bq, Wk, bk, Wv, bv, Wo, bo):
        import jax, jax.numpy as jnp
        import numpy as np
        D_MODEL = 256
        N_HEADS = 16
        D_HEAD = D_MODEL // N_HEADS
        SEQ = 512
        BATCH = 2
        B, S, D = x.shape
        H, Dh = (N_HEADS, D_HEAD)
        q = (x @ Wq + bq).reshape(B, S, H, Dh).transpose(0, 2, 1, 3)
        k = (x @ Wk + bk).reshape(B, S, H, Dh).transpose(0, 2, 1, 3)
        v = (x @ Wv + bv).reshape(B, S, H, Dh).transpose(0, 2, 1, 3)
        scores = jnp.einsum('bhqd,bhkd->bhqk', q, k) / jnp.sqrt(jnp.float32(Dh))
        causal = jnp.tril(jnp.ones((S, S), dtype=bool))
        scores = jnp.where(causal[None, None], scores, jnp.float32(-jnp.inf))
        attn = jax.nn.softmax(scores, axis=-1)
        h = jnp.einsum('bhqk,bhkd->bhqd', attn, v)
        h = h.transpose(0, 2, 1, 3).reshape(B, S, D)
        return h @ Wo + bo

    def _L0_xattn_ref(query, key, value, mask, Wq, Wk, Wv, Wo, bo):
        import jax, jax.numpy as jnp
        import numpy as np
        EMBED = 256
        HEADS = 16
        HEAD_DIM = EMBED // HEADS
        N, Q, _ = query.shape
        K = key.shape[1]
        q = query.reshape(N, Q, HEADS, HEAD_DIM)
        k = key.reshape(N, K, HEADS, HEAD_DIM)
        v = value.reshape(N, K, HEADS, HEAD_DIM)
        q = jnp.einsum('nqhd,ed->nqhe', q, Wq)
        k = jnp.einsum('nkhd,ed->nkhe', k, Wk)
        v = jnp.einsum('nkhd,ed->nkhe', v, Wv)
        energy = jnp.einsum('nqhd,nkhd->nhqk', q, k)
        energy = jnp.where(mask == 0, jnp.float32(-1e+20), energy)
        attn = jax.nn.softmax(energy / jnp.sqrt(jnp.float32(EMBED)), axis=3)
        out = jnp.einsum('nhqk,nkhd->nqhd', attn, v).reshape(N, Q, EMBED)
        return out @ Wo.T + bo

    def _L0_ffn_ref(hidden_states, norm_w, Wg, Wq, Wk, Wv, Wf, gnorm_w, Wo):
        import jax, jax.numpy as jnp
        import numpy as np
        B, S = (2, 256)
        E, TOPK = (8, 2)
        HIDDEN, HEADS, NSLOTS = (256, 4, 64)
        HEAD_K = HIDDEN // HEADS
        HEAD_V = HIDDEN // HEADS
        GATE_NORM = 8.0
        SCALE = 1.0
        EPS = 1e-05
        CHUNK = 64
        CAP = S

        def rms_norm(x, w, eps=EPS):
            y = x * jax.lax.rsqrt(jnp.mean(x * x, axis=-1, keepdims=True) + eps)
            return y * w

        def swish(x):
            return x * jax.nn.sigmoid(x)

        def gsa_chunk(q, k, v, s, g):
            EBH = q.shape[:3]
            T, Dk, Dv, M = (q.shape[3], q.shape[-1], v.shape[-1], s.shape[-1])
            Nc = T // CHUNK

            def to_chunks(x):
                return jnp.moveaxis(x.reshape(EBH + (Nc, CHUNK, x.shape[-1])), 3, 0)
            qc, kc, vc, sc, gc = map(to_chunks, (q, k, v, s, g))
            Gc = jnp.cumsum(gc, axis=-2)
            tril = jnp.tril(jnp.ones((CHUNK, CHUNK), q.dtype))
            hk0 = jnp.zeros(EBH + (Dk, M), q.dtype)
            hv0 = jnp.zeros(EBH + (M, Dv), q.dtype)

            def step(carry, xs):
                hk, hv = carry
                qt, kt, vt, st, Gt = xs
                dec = jnp.exp(Gt)
                s_in = st * jnp.exp(-Gt)
                A = jnp.einsum('ebhik,ebhjk->ebhij', qt, kt) * SCALE * tril
                ok = dec * (jnp.einsum('ebhij,ebhjm->ebhim', A, s_in) + SCALE * jnp.einsum('ebhik,ebhkm->ebhim', qt, hk))
                qv = jax.nn.softmax(ok, axis=-1)
                qvg = qv * dec
                Tm = jnp.einsum('ebhim,ebhjm->ebhij', qvg, s_in) * tril
                ov = jnp.einsum('ebhij,ebhjd->ebhid', Tm, vt) + jnp.einsum('ebhim,ebhmd->ebhid', qvg, hv)
                gl = jnp.exp(Gt[..., -1, :])
                s_rem = st * jnp.exp(Gt[..., -1:, :] - Gt)
                hk = hk * gl[..., None, :] + jnp.einsum('ebhck,ebhcm->ebhkm', kt, s_rem)
                hv = hv * gl[..., :, None] + jnp.einsum('ebhcm,ebhcd->ebhmd', s_rem, vt)
                return ((hk, hv), ov)
            _, ov = jax.lax.scan(step, (hk0, hv0), (qc, kc, vc, sc, Gc))
            return jnp.moveaxis(ov, 0, 3).reshape(EBH + (T, Dv))

        def forward(hidden_states, norm_w, Wg, Wq, Wk, Wv, Wf, gnorm_w, Wo):
            b, s, d = hidden_states.shape
            x = rms_norm(hidden_states, norm_w)
            scores = jax.nn.softmax(jnp.einsum('bsd,ed->bse', x, Wg), axis=-1)
            rw, sel = jax.lax.top_k(scores, TOPK)
            rw = rw / jnp.sum(rw, axis=-1, keepdims=True)
            routing_mask = jax.nn.one_hot(sel, E, dtype=jnp.int32).sum(2)
            s_eff = s * TOPK
            xr = jnp.repeat(x, TOPK, axis=1).reshape(b * s_eff, d)
            batch_idx = jnp.repeat(jnp.arange(b), s_eff)
            combined = batch_idx * E + sel.reshape(-1)
            sorted_indices = jnp.argsort(combined)
            x_sorted = xr[sorted_indices]
            counts = routing_mask.sum(1)
            flat_end = (jnp.cumsum(counts, axis=1) + jnp.arange(b)[:, None] * s_eff).reshape(-1)
            start = jnp.concatenate([jnp.zeros((1,), flat_end.dtype), flat_end[:-1]])
            pos = jnp.arange(CAP)[None, :] + start[:, None]
            trunc = pos + counts.reshape(-1)[:, None] - CAP
            mask = (trunc < flat_end[:, None]) & (trunc >= 0) & (trunc >= start[:, None])
            trunc = jnp.where(mask, trunc, 0)
            xe = x_sorted[trunc.reshape(-1)].reshape(b * E, CAP, d) * mask[..., None]
            xe = xe.reshape(b, E, CAP, d).transpose(1, 0, 2, 3)
            q = jnp.einsum('ebtd,kd->ebtk', xe, Wq).reshape(E, b, CAP, HEADS, HEAD_K)
            k = jnp.einsum('ebtd,ekd->ebtk', xe, Wk).reshape(E, b, CAP, HEADS, HEAD_K)
            v = jnp.einsum('ebtd,ekd->ebtk', xe, Wv).reshape(E, b, CAP, HEADS, HEAD_V)
            f = jnp.einsum('ebtd,ekd->ebtk', xe, Wf).reshape(E, b, CAP, HEADS, NSLOTS)
            g = jax.nn.log_sigmoid(f) / GATE_NORM
            slot = 1.0 - jnp.exp(g)
            q, k = (swish(q), swish(k))
            tr = lambda a: a.transpose(0, 1, 3, 2, 4)
            o = gsa_chunk(tr(q), tr(k), tr(v), tr(slot), tr(g)).transpose(0, 1, 3, 2, 4)
            gathered = o.transpose(1, 0, 2, 3, 4).reshape(b * E * CAP, HEADS, HEAD_V)
            gathered = gathered * mask.reshape(-1)[:, None, None]
            resort = jnp.zeros((b * s_eff, HEADS, HEAD_V), gathered.dtype).at[trunc.reshape(-1)].add(gathered)
            restored = resort[jnp.argsort(sorted_indices)].reshape(b, s, TOPK, HEADS, HEAD_V)
            out = (restored * rw[..., None, None]).sum(2).reshape(b, s, HIDDEN)
            return jnp.einsum('bsd,od->bso', rms_norm(out, gnorm_w), Wo)
        return forward(hidden_states, norm_w, Wg, Wq, Wk, Wv, Wf, gnorm_w, Wo)
    x = x + _L0_attn_ref(_layernorm(x, axis=-1), L0_attn_Wq, L0_attn_bq, L0_attn_Wk, L0_attn_bk, L0_attn_Wv, L0_attn_bv, L0_attn_Wo, L0_attn_bo)
    x = x + _L0_xattn_ref(_layernorm(x, axis=-1), ctx_1024, ctx_1024, mask_Bx1xSxS2_ik1, L0_xattn_Wq, L0_xattn_Wk, L0_xattn_Wv, L0_xattn_Wo, L0_xattn_bo)
    x = x + _L0_ffn_ref(_layernorm(x, axis=-1), L0_ffn_norm_w, L0_ffn_Wg, L0_ffn_Wq, L0_ffn_Wk, L0_ffn_Wv, L0_ffn_Wf, L0_ffn_gnorm_w, L0_ffn_Wo)
    return x

_drawn_inputs = setup_inputs


def setup_inputs(seed=0):
    import zlib

    import numpy as np

    out = dict(_drawn_inputs(seed))
    spreads = {'L0_xattn_bo': (0.0, 0.1), 'L0_ffn_norm_w': (1.0, 0.2), 'L0_ffn_gnorm_w': (1.0, 0.2)}
    factors = {'L0_attn_bq': 8.0, 'L0_attn_bk': 8.0, 'L0_ffn_Wq': 8.0, 'L0_ffn_Wk': 8.0, 'L0_ffn_Wf': 8.0}
    for name, (base, spread) in spreads.items():
        noise = np.random.default_rng([zlib.crc32(name.encode()), seed]).standard_normal(out[name].shape)
        drawn = base * np.exp(spread * noise) if base else spread * noise
        out[name] = jnp.asarray(drawn.astype(out[name].dtype))
    for name, factor in factors.items():
        out[name] = (out[name] * factor).astype(out[name].dtype)
    return out
```

```python
import concourse.bass as bass
from concourse import mybir
from contextlib import ExitStack

NB, S, D, NK = 8, 112, 256, 375
KC, NC3 = 125, 3
NE, NT = 8, 21
NSLOT = NT * 128
WC = 2 * 768
C_ID, C_LE, C_LC, C_GT, C_LT, C_BD, C_BD2, C_HM, C_PR, C_SL, C_TH, C_CB = (
    0, 128, 256, 384, 512, 640, 768, 896, 904, 968, 989, 996)
C_N = C_CB + 112


class Queue:

    def __init__(self, sem):
        self.sem, self.n, self.items = sem, 0, []

    def put(self, fn, *waits, sig=True):
        self.items.append((fn, [w for w in waits if w is not None], sig))
        if sig:
            self.n += 1
            return (self.sem, self.n)
        return None

    def dma(self, fn, sem, *waits):
        sem[1] += 16
        self.items.append((fn, [w for w in waits if w is not None], sem[0]))
        return (sem[0], sem[1])

    def play(self, eng):
        seen = {}
        for fn, waits, sig in self.items:
            for s, v in waits:
                if seen.get(id(s), 0) < v:
                    eng.wait_ge(s, v)
                    seen[id(s)] = v
            ins = fn(eng)
            if sig is True:
                ins.then_inc(self.sem, 1)
            elif sig is not False:
                ins.then_inc(sig, 16)


def decoder_kernel(nc, x, ctx, ctxT, mask, wself, bself, wxq, wxk, wxv, wxo, rows, wg, wmoe, wq_moe, wo_moe,
                   consts, out):
    f32, bf16, i32 = mybir.dt.float32, mybir.dt.bfloat16, mybir.dt.int32
    ALU, ACT, AX = mybir.AluOpType, mybir.ActivationFunctionType, mybir.AxisListType
    X = AX.X
    root = ExitStack()
    with root:
        def sbuf(stack, name, shape, dt=f32):
            return stack.enter_context(nc.sbuf_tensor(name, shape, dt))

        def semaphore(name):
            return root.enter_context(nc.semaphore(name))

        PE, DVE, ACTE, POOL, SP = (Queue(semaphore(n)) for n in ("q_pe", "q_dve", "q_act", "q_pool", "q_sp"))
        dsem = lambda name: [semaphore(name), 0]
        T = {}

        def W(*key):
            return T.get(key)

        ps = root.enter_context(nc.psum_tensor("ps", [128, 8, 512], f32))
        bank_free = {}

        cst = sbuf(root, "cst", [128, C_N])
        xbo = sbuf(root, "xbo", [S, NB, D])
        y = sbuf(root, "y", [S, NB, D])
        wm = sbuf(root, "wm", [128, NE * WC])
        wqm = sbuf(root, "wqm", [128, 2, 256])
        wom = sbuf(root, "wom", [128, 2, 256])
        rw_sb = sbuf(root, "rw_sb", [S, 5, 256])
        lg = sbuf(root, "lg", [S, NB, NE])
        st = sbuf(root, "st", [S, NB, 3, 12])
        epow = sbuf(root, "epow", [S, 1])
        zer = sbuf(root, "zer", [128, 256])
        rwt_ = sbuf(root, "rwt", [S, 2, NB])
        idx_ = sbuf(root, "idx", [S, 2, NB], i32)
        segc_ = sbuf(root, "segc", [128, NT])
        et1_ = sbuf(root, "et1", [1, NT])
        eti_ = sbuf(root, "eti", [1, NT], i32)
        one_ = sbuf(root, "one_", [S, 128])
        one64_128 = one_[:, :]
        ident = cst[:, C_ID:C_ID + 128]
        x2 = xbo
        xs_d = nc.dram_tensor("xs_d", [NSLOT, 256], f32)
        o_d = nc.dram_tensor("o_d", [NSLOT, 256], f32)

        att = ExitStack()
        ws = sbuf(att, "ws", [128, 4, 2, 256])
        bqk = sbuf(att, "bqk", [128, 4])
        wxq_s = sbuf(att, "wxq_s", [16, 128])
        wxk_s = sbuf(att, "wxk_s", [16, 128])
        wxv_s = sbuf(att, "wxv_s", [128, 128])
        wxo_s = sbuf(att, "wxo_s", [128, 2, 256])
        wg_s = sbuf(att, "wg_s", [128, 2, NE])
        bdq = sbuf(att, "bdq", [128, 128])
        bdv = sbuf(att, "bdv", [128, 128])
        fo = sbuf(att, "fo", [128, 2, 256])
        idb = sbuf(att, "idb", [S, S], bf16)
        cmb = sbuf(att, "cmb", [S, 4, S], bf16)
        hmq = sbuf(att, "hmq", [128, 8, S])
        mki = sbuf(att, "mki", [S, 2, NK], i32)
        mkb = sbuf(att, "mkb", [S, NB, NK], bf16)
        cx = sbuf(att, "cx", [KC, 3, NC3, D])
        cxT = sbuf(att, "cxT", [128, 3, 2, NK])
        xn = sbuf(att, "xn", [S, 2, D])
        xnT = sbuf(att, "xnT", [128, 2, 2, S])
        qk = sbuf(att, "qk", [128, 2, 4, S])
        va = sbuf(att, "va", [S, 2, 16, 17])
        qz = sbuf(att, "qz", [128, 3, 2, 8, S])
        qx = sbuf(att, "qx", [128, 2, S])
        PR = 3
        pr = sbuf(att, "pr", [S, PR, 2, NK])
        pt = sbuf(att, "pt", [KC, PR, 2 * NC3, S])
        mx = sbuf(att, "mx", [S, NB, 2, 16])
        sm = sbuf(att, "sm", [S, 2, 16])
        on = sbuf(att, "on", [S, 2, D])
        onT = sbuf(att, "onT", [128, 2, 2, S])
        sq = sbuf(att, "sq", [S, D])
        x1 = sbuf(att, "x1", [S, 2, D])

        def load(name, dst, src, q=SP, *waits):
            T[name] = q.dma(lambda e: e.dma_start(dst, src), dsem("l_" + name), *waits)

        load("cst", cst[:, :], consts)
        load("x", xbo[:, :, :], x.rearrange("b s d -> s b d"))
        load("rows", rw_sb[:, :, :].rearrange("p a n -> p (a n)"), rows.partition_broadcast(S))
        load("ws", ws[:, :, :, :], wself.rearrange("w (t p) n -> p w t n", p=128))
        load("bqk", bqk[:, :], bself)
        d_mk = [dsem("d_mk0"), dsem("d_mk1")]
        d_cx = [dsem(f"d_cx{i}") for i in range(3)]
        d_ct = [dsem(f"d_ct{i}") for i in range(3)]
        cxr = ctx.rearrange("b (c p) d -> b p c d", p=KC)

        def load_mask(b):
            T["mki", b] = SP.dma(lambda e: e.dma_start(mki[:, b % 2, :], mask[b, 0, :, :]), d_mk[b % 2], W("mkb", b - 2))

        def load_ctx(b):
            T["cx", b] = SP.dma(lambda e: e.dma_start(cx[:, b % 3, :, :], cxr[b]), d_cx[b % 3], W("pv", "c", b - 3))
            T["cxT", b] = SP.dma(lambda e: e.dma_start(cxT[:, b % 3, :, :], ctxT[b].rearrange("(t p) k -> p t k", p=128)),
                                 d_ct[b % 3], W("pv", "c", b - 3))

        load_mask(0)
        load("wxq", wxq_s[:, :], wxq)
        load("wxk", wxk_s[:, :], wxk)
        load("wxv", wxv_s[:, :], wxv)
        load("wxo", wxo_s[:, :, :], wxo.rearrange("(t p) n -> p t n", p=128))
        load("wg", wg_s[:, :, :], wg.rearrange("(t p) n -> p t n", p=128))
        load_ctx(0)
        load_mask(1)
        load_ctx(1)
        load_ctx(2)
        load("wqm", wqm[:, :, :], wq_moe.rearrange("(t p) n -> p t n", p=128))
        load("wom", wom[:, :, :], wo_moe.rearrange("(t p) n -> p t n", p=128))
        for e8 in range(NE):
            load(f"wm{e8}", wm[:, e8 * WC:(e8 + 1) * WC].rearrange("p (t n) -> p t n", t=2),
                 wmoe[e8].rearrange("(t p) n -> p t n", p=128))

        T["zer"] = POOL.put(lambda e: e.memset(zer[:, :], 0.0))
        T["epow"] = POOL.put(lambda e: e.memset(epow[:, :], -0.5))
        T["ones"] = POOL.put(lambda e: e.memset(one_[:, :], 1.0))
        T["vone"] = POOL.put(lambda e: e.memset(va[:, :, :, 16:17], 1.0))
        T["hmq"] = POOL.put(lambda e: e.tensor_copy(
            hmq[:, :, :], cst[:, C_HM:C_HM + 8].unsqueeze(2).to_broadcast([128, 8, S])), T["cst"])
        T["idb"] = DVE.put(lambda e: e.tensor_copy(idb[:, :], cst[0:S, C_ID:C_ID + S]), T["cst"])
        T["cmb"] = DVE.put(lambda e: e.tensor_copy(
            cmb[:, :, :], cst[0:S, C_CB:C_CB + S].unsqueeze(1).to_broadcast([S, 4, S])))
        zsem = dsem("zsem")
        for i in range(NT):
            T["zero"] = SP.dma(lambda e, i=i: e.dma_start(xs_d[128 * i:128 * i + 128, :], zer[:, :]), zsem, T["zer"])

        def mm(o, l, r, start, stop, *waits, sig=False):
            return PE.put(lambda e: e.matmul(o, l, r, start=start, stop=stop), *waits, sig=sig)

        def tr(o, i, n, *waits, sig=False):
            return PE.put(lambda e: e.transpose(o, i, ident[0:n, 0:n]), *waits, sig=sig)

        mm(ps[:, 7, 0:128], wxq_s[:, :], wxk_s[:, :], True, True, T["wxq"], T["wxk"])
        T["bdq_p"] = mm(ps[:, 7, 0:128], wxq_s[:, :], wxk_s[:, :], True, True, sig=True)
        T["bdq"] = DVE.put(lambda e: e.tensor_tensor(bdq[:, :], ps[:, 7, 0:128], cst[:, C_BD:C_BD + 128], ALU.mult),
                           T["bdq_p"])
        T["bdv"] = DVE.put(lambda e: e.tensor_tensor(bdv[:, :], wxv_s[:, :], cst[:, C_BD:C_BD + 128], ALU.mult),
                           T["wxv"])
        for t in range(2):
            T["fo_p"] = mm(ps[:, 7, 256 * t:256 * t + 256], bdv[:, :], wxo_s[:, t, :], True, True,
                           T["bdv"], T["bdq"], T["wxo"], sig=True)
        T["fo"] = DVE.put(lambda e: e.tensor_copy(fo[:, :, :].rearrange("p t n -> p (t n)"), ps[:, 7, :]), T["fo_p"])
        bank_free[7] = T["fo"]

        def ln_stats(src, b, j, *waits):
            v = st[:, b, j, :]
            a = DVE.put(lambda e: e.bn_stats(v[:, 0:6], src), *waits)
            a = DVE.put(lambda e: e.bn_aggr(v[:, 6:8], v[:, 0:6]), a)
            a = POOL.put(lambda e: e.tensor_scalar(v[:, 8:9], v[:, 7:8], 1e-5, None, ALU.add), a, T["epow"])
            return POOL.put(lambda e: e.tensor_tensor(v[:, 9:10], v[:, 8:9], epow[:, :], ALU.pow), a)

        def ln_apply(dst, src, b, j, *waits):
            v = st[:, b, j, :]
            return DVE.put(lambda e: e.tensor_scalar(dst, src, v[:, 6:7], v[:, 9:10], ALU.subtract, ALU.mult), *waits)

        def make_xn(kind, b):
            j = 0 if kind == "s" else 1
            src = xbo[:, b, :] if kind == "s" else x1[:, b % 2, :]
            pre = T["x"] if kind == "s" else T["x1", b]
            a = ln_stats(src, b, j, pre)
            T["xn", kind, b] = ln_apply(xn[:, b % 2, :], src, b, j, a, W("xn_free", b % 2))
            if kind == "s":
                T["xbo", b] = POOL.put(lambda e: e.tensor_tensor(xbo[:, b, :], xbo[:, b, :], rw_sb[:, 1, :], ALU.add),
                                       T["xn", kind, b], T["rows"])

        def transpose2(key, src, dstname, dst, b, *waits):
            for t in range(2):
                a = tr(ps[:, 7, S * t:S * t + S], src[:, 128 * t:128 * t + 128], S, bank_free[7], T["cst"], *waits,
                       sig=t == 1)
            T[key + "_tr", b] = a
            r = ACTE.put(lambda e: e.activation(dst.rearrange("p t n -> p (t n)"), ps[:, 7, 0:2 * S], ACT.Copy), a,
                         W(dstname + "_free", b % 2))
            bank_free[7] = r
            return r

        def make_xnT(kind, b):
            T["xnT", kind, b] = transpose2("xnT" + kind, xn[:, b % 2, :], "xnT", xnT[:, b % 2, :, :], b,
                                           T["xn", kind, b])
            T["xn_free", b % 2] = T["xnT" + kind + "_tr", b]

        def self_qk(b):
            for w in range(2):
                for m in range(2):
                    for t in range(2):
                        a = mm(ps[:, 7, (2 * w + m) * S:(2 * w + m + 1) * S], ws[:, w, t, 128 * m:128 * m + 128],
                               xnT[:, b % 2, t, :], t == 0, t == 1, bank_free[7], T["xnT", "s", b], T["ws"],
                               sig=(w, m, t) == (1, 1, 1))
            r = DVE.put(lambda e: e.tensor_tensor(qk[:, b % 2, :, :], ps[:, 7, 0:4 * S].rearrange("p (a n) -> p a n", a=4),
                                                  bqk[:, :].unsqueeze(2).to_broadcast([128, 4, S]), ALU.add),
                        a, T["bqk"], W("st", "s", b - 2), W("qz", "s", b - 2))
            T["qk", b] = bank_free[7] = r

        def self_v(b):
            for t in range(2):
                a = mm(ps[0:S, 7, 0:256], xnT[:, b % 2, t, :], ws[:, 2, t, :], t == 0, t == 1, bank_free[7],
                       T["xnT", "s", b], sig=t == 1)
            T["xnT_free", b % 2] = a
            r = DVE.put(lambda e: e.tensor_tensor(
                va[:, b % 2, :, 0:16], ps[0:S, 7, 0:256].rearrange("p (h n) -> p h n", h=16),
                rw_sb[:, 0, :].rearrange("p (h n) -> p h n", h=16), ALU.add), a, T["rows"], T["vone"],
                W("pv", "s", b - 2))
            T["va", b] = bank_free[7] = r

        def make_qz(kind, b):
            k = 0 if kind == "s" else 1 + b % 2
            for t in range(2):
                src = qk[:, b % 2, t, :] if kind == "s" else qx[:, t, :]
                pre = T["qk", b] if kind == "s" else T["qx", b]
                a = POOL.put(lambda e, src=src, t=t: e.tensor_tensor(
                    qz[:, k, t, :, :], src.unsqueeze(1).to_broadcast([128, 8, S]), hmq[:, :, :], ALU.mult),
                    pre, T["hmq"], W("st", kind, b - 1 if kind == "s" else b - 2))
            T["qz", kind, b] = a

        def cross_q(b):
            for t in range(2):
                a = mm(ps[:, 7, S * t:S * t + S], bdq[:, :], xnT[:, b % 2, t, :], True, True, bank_free[7],
                       T["xnT", "c", b], T["bdq"], sig=t == 1)
            T["xnT_free", b % 2] = a
            r = ACTE.put(lambda e: e.activation(qx[:, :, :].rearrange("p t n -> p (t n)"), ps[:, 7, 0:2 * S], ACT.Copy),
                         a, W("qz", "c", b - 1))
            T["qx", b] = bank_free[7] = r

        def mask_bias(b):
            T["mkb", b] = DVE.put(lambda e: e.tensor_scalar(mkb[:, b, :], mki[:, b % 2, :], 0.0, -1e20,
                                                            ALU.is_equal, ALU.mult), T["mki", b])
            if b + 2 < NB:
                load_mask(b + 2)

        def normed(kind, b):
            o17 = ps[0:S, 6, 0:272].rearrange("p (h n) -> p h n", h=16)
            if kind == "s":
                a = DVE.put(lambda e: e.reciprocal(sm[:, 0, :], o17[:, :, 16]), T["pv", "s", b])
                src = o17[:, :, 0:16]
            else:
                a = DVE.put(lambda e: e.reciprocal(sm[:, 1, :], mx[:, b, 1, :]), T["pv", "c", b])
                src = ps[0:S, 6, 0:256].rearrange("p (h n) -> p h n", h=16)
            k = 0 if kind == "s" else 1
            r = DVE.put(lambda e: e.tensor_tensor(
                on[:, k, :].rearrange("p (h n) -> p h n", h=16), src,
                sm[:, k, :].unsqueeze(2).to_broadcast([S, 16, 16]), ALU.mult), a, W("on_free", k))
            T["on", kind, b] = bank_free[6] = r

        def make_onT(kind, b):
            k = 0 if kind == "s" else 1
            T["onT", kind, b] = transpose2("onT" + kind, on[:, k, :], "onT" + kind, onT[:, k, :, :], b,
                                           T["on", kind, b], )
            T["on_free", k] = T["onT" + kind + "_tr", b]

        def out_proj(kind, b):
            k = 0 if kind == "s" else 1
            for t in range(2):
                w = ws[:, 3, t, :] if kind == "s" else fo[:, t, :]
                a = mm(ps[0:S, 7, 0:256], onT[:, k, t, :], w, t == 0, t == 1, bank_free[7], T["onT", kind, b],
                       T["fo"], sig=t == 1)
            T["onT" + kind + "_free", 0] = T["onT" + kind + "_free", 1] = a
            if kind == "s":
                r = DVE.put(lambda e: e.tensor_tensor(x1[:, b % 2, :], ps[0:S, 7, 0:256], xbo[:, b, :], ALU.add), a,
                            T["xbo", b], W("x1b", b - 2))
                T["x1", b] = bank_free[7] = r
            else:
                T["x2", b] = bank_free[7] = DVE.put(lambda e: e.tensor_tensor(
                    x2[:, b, :], ps[0:S, 7, 0:256], x2[:, b, :], ALU.add), a, T["x1b", b])

        def x1_bias(b):
            T["x1b", b] = POOL.put(lambda e: e.tensor_tensor(x2[:, b, :], x1[:, b % 2, :], rw_sb[:, 2, :], ALU.add),
                                   T["x1", b], T["xn", "c", b])

        def ffn_norm1(b):
            a = ln_stats(x2[:, b, :], b, 2, T["x2", b])
            T["xh", b] = ln_apply(y[:, b, :], x2[:, b, :], b, 2, a)
            v = st[:, b, 2, :]
            a = ACTE.put(lambda e: e.activation(sq[:, :], y[:, b, :], ACT.Square, accum_out=v[:, 10:11]), T["xh", b],
                         W("sq", b - 1))
            T["sq", b] = a
            a = POOL.put(lambda e: e.tensor_scalar(v[:, 8:9], v[:, 10:11], 1.0 / D, 1e-5, ALU.mult, ALU.add), a)
            T["rr", b] = POOL.put(lambda e: e.tensor_tensor(v[:, 11:12], v[:, 8:9], epow[:, :], ALU.pow), a)

        def ffn_norm2(b):
            v = st[:, b, 2, :]
            T["y", b] = DVE.put(lambda e: e.scalar_tensor_tensor(y[:, b, :], y[:, b, :], v[:, 11:12], rw_sb[:, 3, :],
                                                                 ALU.mult, ALU.mult), T["rr", b], T["xh", b])

        def ffn_yT(b):
            T["yT", b] = transpose2("yT", y[:, b, :], "onTc", onT[:, 1, :, :], b, T["y", b])

        def ffn_logits(b):
            for t in range(2):
                a = mm(ps[0:S, 7, 0:NE], onT[:, 1, t, :], wg_s[:, t, :], t == 0, t == 1, bank_free[7], T["yT", b],
                       T["wg"], sig=t == 1)
            T["onTc_free", 0] = T["onTc_free", 1] = a
            T["lg", b] = bank_free[7] = DVE.put(lambda e: e.tensor_copy(lg[:, b, :], ps[0:S, 7, 0:NE]), a)

        units = []
        side = {}

        def add_units(kind, b):
            for g in range(4 if kind == "s" else 8):
                units.append((kind, b, g))

        def unit_scores(n):
            kind, b, g = units[n]
            bk = 2 * (n % 2)
            if kind == "s":
                out4 = ps[0:S, bk, 0:4 * S]
                mm(out4, idb[:, :], cmb[:, :, :].rearrange("p a n -> p (a n)"), True, False, bank_free.get(bk),
                   bank_free.get(bk + 1), T["idb"], T["cmb"])
                for i in range(4):
                    h = 4 * g + i
                    a = mm(ps[0:S, bk, S * i:S * i + S], qz[:, 0, h // 8, h % 8, :], qk[:, b % 2, 2 + h // 8, :],
                           False, i == 3, T["qz", kind, b], T["qk", b], sig=i == 3)
            else:
                for i in range(2):
                    h = 2 * g + i
                    mm(ps[0:S, bk + i, 0:NK], idb[:, :], mkb[:, b, :], True, False, bank_free.get(bk),
                       bank_free.get(bk + 1), T["mkb", b])
                    a = mm(ps[0:S, bk + i, 0:NK], qz[:, 1 + b % 2, h // 8, h % 8, :], cxT[:, b % 3, h // 8, :],
                           False, True, T["qz", kind, b], T["cxT", b], sig=i == 1)
            T["E", n] = a
            T["st", kind, b] = a

        def unit_soft(n):
            kind, b, g = units[n]
            bk, r = 2 * (n % 2), n % PR
            if kind == "s":
                src = ps[0:S, bk, 0:4 * S].rearrange("p (h n) -> p h n", h=4)
                m4 = mx[:, b, 0, 4 * g:4 * g + 4]
                a = DVE.put(lambda e: e.tensor_reduce(m4, src, axis=X, op=ALU.max), T["E", n])
                dst = pr[:, r, :, :].rearrange("p a n -> p (a n)")[:, 0:4 * S]
                a = DVE.put(lambda e: e.tensor_tensor(dst.rearrange("p (h n) -> p h n", h=4), src,
                                                      m4.unsqueeze(2).to_broadcast([S, 4, S]), ALU.subtract),
                            a, W("T", n - PR))
                bank_free[bk] = bank_free[bk + 1] = a
                T["P", n] = ACTE.put(lambda e: e.activation(dst, dst, ACT.Exp, scale=0.25), a)
            else:
                m2 = mx[:, b, 0, 2 * g:2 * g + 2]
                a = DVE.put(lambda e: e.tensor_reduce(m2, ps[0:S, bk:bk + 2, 0:NK], axis=X, op=ALU.max), T["E", n],
                            W("ngm", n))
                a = DVE.put(lambda e: e.tensor_scalar(m2, m2, -0.0625, None, ALU.mult), a)
                for i in range(2):
                    T["P", n] = ACTE.put(lambda e, i=i: e.activation(
                        pr[:, r, i, :], ps[0:S, bk + i, 0:NK], ACT.Exp, bias=mx[:, b, 0, 2 * g + i:2 * g + i + 1],
                        scale=0.0625, accum_out=mx[:, b, 1, 2 * g + i:2 * g + i + 1]), a, W("T", n - PR))
                bank_free[bk] = bank_free[bk + 1] = T["P", n]

        def unit_transpose(n):
            kind, b, g = units[n]
            r = n % PR
            if kind == "s":
                flat = pr[:, r, :, :].rearrange("p a n -> p (a n)")
                for i in range(4):
                    a = tr(ps[0:S, 4, S * i:S * i + S], flat[:, S * i:S * i + S], S, T["P", n], bank_free.get(4),
                           sig=i == 3)
                T["T", n] = a
                T["pt", n] = bank_free[4] = DVE.put(lambda e: e.tensor_copy(
                    pt[0:S, r, 0:4, :].rearrange("p a n -> p (a n)"), ps[0:S, 4, 0:4 * S]), a, W("PV", n - PR))
            else:
                for i in range(2):
                    for c in range(NC3):
                        a = tr(ps[0:KC, 4 + i, S * c:S * c + S], pr[:, r, i, KC * c:KC * c + KC], S, T["P", n],
                               bank_free.get(4 + i), sig=c == NC3 - 1)
                    dst = pt[:, r, NC3 * i:NC3 * i + NC3, :].rearrange("p a n -> p (a n)")
                    src = ps[0:KC, 4 + i, 0:NC3 * S]
                    if i == 0:
                        bank_free[4] = t0 = DVE.put(lambda e, d=dst, s=src: e.tensor_copy(d, s), a, W("PV", n - PR))
                    else:
                        bank_free[5] = t1 = DVE.put(lambda e, d=dst, s=src: e.tensor_copy(d, s), a,
                                                    W("PV", n - PR))
                T["T", n] = a
                T["pt", n] = t1

        def unit_pv(n):
            kind, b, g = units[n]
            r = n % PR
            if kind == "s":
                for i in range(4):
                    h = 4 * g + i
                    a = mm(ps[0:S, 6, 17 * h:17 * h + 17], pt[0:S, r, i, :], va[:, b % 2, h, :], True, True,
                           T["pt", n], T["va", b], bank_free.get(6), sig=i == 3)
            else:
                for i in range(2):
                    h = 2 * g + i
                    for c in range(NC3):
                        a = mm(ps[0:S, 6, 16 * h:16 * h + 16], pt[:, r, NC3 * i + c, :],
                               cx[:, b % 3, c, 16 * h:16 * h + 16], c == 0, c == NC3 - 1,
                               T["pt", n], T["cx", b], bank_free.get(6), sig=(i, c) == (1, NC3 - 1))
            T["PV", n] = a
            T["pv", kind, b] = a
            if (kind == "s" and g == 3) or (kind == "c" and g == 7):
                normed(kind, b)
                if kind == "c" and b + 3 < NB:
                    load_ctx(b + 3)

        def prologue(b):
            return [lambda: make_xn("s", b), lambda: make_xnT("s", b), lambda: self_qk(b),
                    lambda: (make_qz("s", b), self_v(b))]

        def middle(b):
            return [lambda: make_onT("s", b), lambda: out_proj("s", b),
                    lambda: make_xn("c", b), lambda: (x1_bias(b), make_xnT("c", b)), lambda: cross_q(b),
                    lambda: make_qz("c", b)]

        def epilogue(b):
            return [lambda: make_onT("c", b), lambda: (out_proj("c", b), ffn_norm1(b)), lambda: ffn_norm2(b),
                    lambda: ffn_yT(b), lambda: ffn_logits(b)]

        for f in prologue(0) + prologue(1)[0:3]:
            f()
        for b in range(2):
            mask_bias(b)
        order = [("s", 0), ("s", 1)]
        for b in range(NB):
            order.append(("c", b))
            if b + 2 < NB:
                order.append(("s", b + 2))
        for kb in order:
            add_units(*kb)
        last_of = {}
        for n, (kind, b, g) in enumerate(units):
            last_of[kind, b] = n
        todo = []
        for n in range(len(units) + 2):
            if n < len(units):
                kind, b, g = units[n]
                if g == 0:
                    for f in todo:
                        f()
                    todo = []
                    if kind == "s" and b == 1:
                        prologue(1)[3]()
                    if kind == "c":
                        todo = (prologue(b + 2) if b + 2 < NB else [])
                        if b + 2 < NB:
                            todo = todo + [lambda b=b: mask_bias(b + 2)]
                unit_scores(n)
                unit_soft(n)
            if 0 <= n - 1 < len(units):
                unit_transpose(n - 1)
            if 0 <= n - 2 < len(units):
                unit_pv(n - 2)
                k2, b2, g2 = units[n - 2]
                if last_of[k2, b2] == n - 2:
                    todo = (middle(b2) if k2 == "s" else epilogue(b2)) + todo
            if todo:
                todo.pop(0)()
        for f in todo:
            f()

        att.close()

        rt = ExitStack()
        R = lambda name, shape, dt=f32: sbuf(rt, name, shape, dt)
        pb = R("pb", [S, NB, NE])
        pc = R("pc", [S, NB, NE])
        m1 = R("m1", [S, NB, NE])
        m2 = R("m2", [S, NB, NE])
        mb = R("mb", [S, NB, NE])
        rd = R("rd", [S, 8, NB])
        cn = R("cn", [128, NB, NE])
        sc = R("sc", [128, NE, NB])
        stt = R("stt", [128, NB, NE])
        e8 = R("e8", [128, 6, NE])
        th = R("th", [128, NE, 7])
        one64 = R("one64", [128, 64])
        seg3 = R("seg3", [128, NT, 64])
        etf = R("etf", [1, NT, NE])
        T["one64"] = POOL.put(lambda e: e.memset(one64[:, :], 1.0))
        rwt, idx, segc, eti, et1 = rwt_, idx_, segc_, eti_, et1_

        def seq(fn, *waits):
            return DVE.put(fn, (DVE.sem, DVE.n), *waits)

        bc8 = lambda a: a.unsqueeze(2).to_broadcast([S, NB, NE])
        lgf = lg[:, :, :]
        seq(lambda e: e.tensor_reduce(rd[:, 0, :], lgf, axis=X, op=ALU.max), T["lg", NB - 1])
        a = seq(lambda e: e.tensor_tensor(pb[:, :, :], lgf, bc8(rd[:, 0, :]), ALU.subtract))
        a = ACTE.put(lambda e: e.activation(pb[:, :, :], pb[:, :, :], ACT.Exp), a)
        seq(lambda e: e.tensor_reduce(rd[:, 1, :], pb[:, :, :], axis=X, op=ALU.add), a)
        seq(lambda e: e.reciprocal(rd[:, 2, :], rd[:, 1, :]))
        seq(lambda e: e.tensor_tensor(pb[:, :, :], pb[:, :, :], bc8(rd[:, 2, :]), ALU.mult))
        prio = cst[0:S, C_PR:C_PR + 64].rearrange("p (b n) -> p b n", b=NB)
        for k, mk in enumerate((m1, m2)):
            seq(lambda e, k=k: e.tensor_reduce(rd[:, 3 + k, :], pb[:, :, :], axis=X, op=ALU.max))
            seq(lambda e, k=k: e.tensor_tensor(pc[:, :, :], pb[:, :, :], bc8(rd[:, 3 + k, :]), ALU.is_equal))
            seq(lambda e: e.tensor_tensor(pc[:, :, :], pc[:, :, :], prio, ALU.mult))
            seq(lambda e: e.tensor_reduce(rd[:, 5, :], pc[:, :, :], axis=X, op=ALU.max))
            seq(lambda e, mk=mk: e.tensor_tensor(mk[:, :, :], pc[:, :, :], bc8(rd[:, 5, :]), ALU.is_equal))
            if k == 0:
                seq(lambda e: e.scalar_tensor_tensor(pb[:, :, :], m1[:, :, :], -4.0, pb[:, :, :], ALU.mult, ALU.add))
        a = seq(lambda e: e.tensor_tensor(mb[:, :, :], m1[:, :, :], m2[:, :, :], ALU.add))
        mbf = mb[:, :, :].rearrange("p b n -> p (b n)")
        mm(ps[0:S, 0, 0:64], cst[0:S, C_LT:C_LT + S], mbf, True, True, a, bank_free[0])
        a = mm(ps[:, 1, 0:64], one64_128, mbf, True, True, a, bank_free[1], T["ones"], sig=True)
        seq(lambda e: e.tensor_tensor(rd[:, 5, :], rd[:, 3, :], rd[:, 4, :], ALU.add))
        seq(lambda e: e.reciprocal(rd[:, 6, :], rd[:, 5, :]))
        for k in range(2):
            T["rwt"] = seq(lambda e, k=k: e.tensor_tensor(rwt[:, k, :], rd[:, 3 + k, :], rd[:, 6, :], ALU.mult))
        seq(lambda e: e.tensor_copy(cn[:, :, :].rearrange("p b n -> p (b n)"), ps[:, 1, 0:64]), a)
        cne = cn[:, :, :].rearrange("p b n -> p n b")
        sc_f = sc[:, :, :].rearrange("p n b -> p (n b)")
        seq(lambda e: e.tensor_reduce(e8[:, 0, :], cne, axis=X, op=ALU.add))
        seq(lambda e: e.tensor_tensor(th[:, :, :], e8[:, 0, :].unsqueeze(2).to_broadcast([128, NE, 7]),
                                      cst[:, C_TH:C_TH + 7].unsqueeze(1).to_broadcast([128, NE, 7]), ALU.is_gt))
        seq(lambda e: e.tensor_reduce(e8[:, 1, :], th[:, :, :], axis=X, op=ALU.add))
        seq(lambda e: e.tensor_tensor_scan(e8[:, 2, :], one64[:, 0:NE], e8[:, 0, :], 0.0, ALU.mult, ALU.add), T["one64"])
        seq(lambda e: e.tensor_tensor_scan(e8[:, 3, :], one64[:, 0:NE], e8[:, 1, :], 0.0, ALU.mult, ALU.add))
        seq(lambda e: e.tensor_tensor(e8[:, 3, :], e8[:, 3, :], e8[:, 1, :], ALU.subtract))
        seq(lambda e: e.tensor_scalar(e8[:, 3, :], e8[:, 3, :], 128.0, None, ALU.mult))
        seq(lambda e: e.tensor_tensor(e8[:, 2, :], e8[:, 2, :], e8[:, 0, :], ALU.subtract))
        seq(lambda e: e.tensor_tensor(e8[:, 4, :], e8[:, 3, :], e8[:, 2, :], ALU.subtract))
        seq(lambda e: e.tensor_copy(sc[:, :, :], cne))
        stf = seg3[:, 0, :]
        seq(lambda e: e.tensor_tensor_scan(stf, one64[:, :], sc_f, 0.0, ALU.mult, ALU.add))
        seq(lambda e: e.tensor_tensor(sc_f, stf, sc_f, ALU.subtract))
        seq(lambda e: e.tensor_tensor(stt[:, :, :].rearrange("p b n -> p n b"), sc[:, :, :],
                                      e8[:, 4, :].unsqueeze(2).to_broadcast([128, NE, NB]), ALU.add))
        seq(lambda e: e.tensor_tensor(pc[:, :, :], stt[0:S, :, :],
                                      ps[0:S, 0, 0:64].rearrange("p (b n) -> p b n", b=NB), ALU.add))
        for k, mk in enumerate((m1, m2)):
            seq(lambda e, mk=mk: e.tensor_tensor(mk[:, :, :], mk[:, :, :], pc[:, :, :], ALU.mult))
            seq(lambda e, mk=mk, k=k: e.tensor_reduce(rd[:, k, :], mk[:, :, :], axis=X, op=ALU.add))
            T["idx"] = seq(lambda e, k=k: e.tensor_copy(idx[:, k, :], rd[:, k, :]))
        bank_free[0] = bank_free[1] = T["idx"]
        xsem = dsem("xsem")
        for b in range(NB):
            for k in range(2):
                T["xs_all"] = POOL.dma(lambda e, b=b, k=k: e.indirect_dma_start(
                    out=xs_d.ap(), out_offset=bass.IndirectOffsetOnAxis(ap=idx[:, k, b:b + 1], axis=0),
                    in_=y[:, b, :], in_offset=None), xsem, T["idx"], T["y", b], T["zero"])
        seq(lambda e: e.tensor_tensor(etf[:, :, :], cst[0:1, C_SL:C_SL + NT].unsqueeze(2).to_broadcast([1, NT, NE]),
                                      e8[0:1, 3, :].unsqueeze(1).to_broadcast([1, NT, NE]), ALU.is_ge))
        seq(lambda e: e.tensor_reduce(et1[:, :], etf[:, :, :], axis=X, op=ALU.add))
        T["eti"] = seq(lambda e: e.tensor_scalar(eti[:, :], et1[:, :], float(WC), -float(WC), ALU.mult, ALU.add))
        seq(lambda e: e.tensor_tensor(
            seg3[:, :, :], cst[:, C_SL:C_SL + NT].unsqueeze(2).to_broadcast([128, NT, 64]),
            stt[:, :, :].rearrange("p b n -> p (b n)").unsqueeze(1).to_broadcast([128, NT, 64]), ALU.is_ge))
        T["segc"] = seq(lambda e: e.tensor_reduce(segc[:, :], seg3[:, :, :], axis=X, op=ALU.add))
        rt.close()

        G = lambda name, shape, dt=f32: sbuf(root, name, shape, dt)
        RX, RV = 2, 4
        xs = G("xs", [128, RX, 256])
        xsT = G("xsT", [128, RX, 256])
        kq = G("kq", [128, 2, 512])
        eq = G("eq", [128, 2, 512])
        vv = G("vv", [128, RV, 256])
        fa = G("fa", [128, 2, 256])
        fm = G("fm", [128, 2, 256])
        ss = G("ss", [128, 2, 256])
        mc = G("mc", [128, RV, 128])
        tcm = G("tcm", [128, 2, 128])
        trm = G("trm", [128, 2, 128])
        pl = G("pl", [128, NT + 1])
        fl = G("fl", [128, 2, NT + 1])
        dc = G("dc", [128, 3, 512])
        ed = G("ed", [128, 2, 256])
        dr = G("dr", [128, 2, 256])
        si = G("si", [128, 3, 256])
        ktz = G("ktz", [128, 2, 4, 128])
        qT = G("qT", [128, 3, 2, 128])
        stz = G("stz", [128, 3, 4, 128])
        am = G("am", [128, 2, 4, 128])
        hz = G("hz", [128, 4, 2, 128])
        hv = G("hv", [128, 4, 2, 128])
        ok = G("ok", [128, 2, 256])
        o2 = G("o2", [128, 2, 256])
        sm4 = G("sm4", [128, 4, 8])
        qg = G("qg", [128, 2, 512])
        qgT = G("qgT", [128, 2, 512])
        tm = G("tm", [128, 2, 4, 128])
        oo = G("oo", [128, 2, 256])
        allt = [T["segc"], T["xs_all"]]
        done_att = (ACTE.sem, ACTE.n), (PE.sem, PE.n), (POOL.sem, POOL.n), (DVE.sem, DVE.n)
        T["z1"] = POOL.put(lambda e: e.memset(ktz[:, :, :, :], 0.0), *done_att, T["idx"])
        T["z2"] = POOL.put(lambda e: e.memset(stz[:, :, :, :], 0.0))
        T["z3"] = POOL.put(lambda e: e.memset(hz[:, 3, :, :], 0.0))
        T["z4"] = POOL.put(lambda e: e.memset(hv[:, 3, :, :], 0.0))
        T["z5"] = POOL.put(lambda e: e.memset(pl[:, 0:1], -1.0))
        T["hz", -1], T["hv", -1], T["pl", -1] = T["z3"], T["z4"], T["z5"]
        le, lc, gt = (cst[:, c:c + 128] for c in (C_LE, C_LC, C_GT))
        bd2 = cst[:, C_BD2:C_BD2 + 128].unsqueeze(1).to_broadcast([128, 2, 128])
        v4 = lambda a: a.rearrange("p (h n) -> p h n", h=4)
        v2 = lambda a: a.rearrange("p (h n) -> p h n", h=2)
        d_xs = [dsem(f"d_xs{i}") for i in range(RX)]

        def bankw(k):
            return bank_free.get(k)

        def g_load(t):
            T["xs", t] = SP.dma(lambda e: e.dma_start(xs[:, t % RX, :], xs_d[128 * t:128 * t + 128, :]), d_xs[t % RX],
                                T["xs_all"], W("xsT_p", t - RX), T["z1"])

        def g_x(t):
            for i in range(2):
                a = tr(ps[:, 0, 128 * i:128 * i + 128], xs[:, t % RX, 128 * i:128 * i + 128], 128, T["xs", t],
                       bankw(0), sig=i == 1)
            T["xsT_p", t] = a
            T["xsT", t] = bank_free[0] = ACTE.put(lambda e: e.activation(xsT[:, t % RX, :], ps[:, 0, 0:256], ACT.Copy),
                                                  a, W("proj", t - RX), T["z1"])
            if t + RX < NT:
                g_load(t + RX)

        def g_proj(t):
            def load_reg(e):
                return e.reg_load(regs[0], eti[0:1, t:t + 1])
            def dyn(o, i, lo, n, start, stop):
                def f(e):
                    off = e.snap(regs[0], min_val=0, max_val=(NE - 1) * WC)
                    return e.matmul(o, xsT[:, t % RX, 128 * i:128 * i + 128],
                                    wm[:, bass.ds(off + (i * 768 + lo), n)], start=start, stop=stop)
                return f
            PE.put(load_reg, T["eti"], T["xsT", t], *(T[f"wm{n}"] for n in range(NE)), sig=False)
            for i in range(2):
                PE.put(dyn(ps[:, 1, 0:256], i, 0, 256, i == 0, i == 1), bankw(1), sig=False)
            for i in range(2):
                a = mm(ps[:, 1, 256:512], xsT[:, t % RX, 128 * i:128 * i + 128], wqm[:, i, :], i == 0, i == 1,
                       T["wqm"], sig=i == 1)
            for i in range(2):
                f = PE.put(dyn(ps[:, 2, 0:512], i, 256, 512, i == 0, i == 1), bankw(2), sig=i == 1)
            T["proj", t] = f
            r = t % 2
            c = ACTE.put(lambda e: e.activation(eq[:, r, :], ps[:, 1, :], ACT.Exp, scale=-1.0), a, W("kq", t - 2))
            c = POOL.put(lambda e: e.tensor_scalar(eq[:, r, :], eq[:, r, :], 1.0, None, ALU.add), c)
            c = DVE.put(lambda e: e.reciprocal(eq[:, r, :], eq[:, r, :]), c)
            T["kq", t] = bank_free[1] = DVE.put(lambda e: e.tensor_tensor(kq[:, r, :], ps[:, 1, :], eq[:, r, :],
                                                                         ALU.mult), c, W("kqT_p", t - 2), W("h_p", t - 2))
            T["vv", t] = ACTE.put(lambda e: e.activation(vv[:, t % RV, :], ps[:, 2, 0:256], ACT.Copy), f,
                                  W("ov", t - RV), W("h_p", t - RV))
            c = ACTE.put(lambda e: e.activation(fa[:, r, :], ps[:, 2, 256:512], ACT.Abs), f, W("ss", t - 2),
                         W("G", t - 2))
            T["fm", t] = DVE.put(lambda e: e.tensor_scalar(fm[:, r, :], ps[:, 2, 256:512], 0.0, None, ALU.min), f, c,
                                 W("G", t - 2), W("ss", t - 2))
            bank_free[2] = T["fm", t]
            c = ACTE.put(lambda e: e.activation(fa[:, r, :], fa[:, r, :], ACT.Exp, scale=-1.0), c)
            c = ACTE.put(lambda e: e.activation(fa[:, r, :], fa[:, r, :], ACT.Ln, bias=1.0), c)
            T["g8", t] = c = POOL.put(lambda e: e.tensor_tensor(fm[:, r, :], fm[:, r, :], fa[:, r, :], ALU.subtract),
                                      c, T["fm", t])
            c = ACTE.put(lambda e: e.activation(ss[:, r, :], fm[:, r, :], ACT.Exp, scale=0.125), c,
                         W("si", t - 2), W("srem", t - 2))
            T["ss", t] = POOL.put(lambda e: e.tensor_scalar(ss[:, r, :], ss[:, r, :], -1.0, 1.0, ALU.mult, ALU.add), c)

        def g_mask(t):
            r = t % 2
            a = tr(ps[:, 0, 0:128], segc[:, t:t + 1].to_broadcast([128, 128]), 128, T["segc"], bankw(0), sig=True)
            row, col = ps[:, 0, 0:128], segc[:, t:t + 1]
            DVE.put(lambda e: e.scalar_tensor_tensor(mc[:, t % RV, :], row, col, le, ALU.is_equal, ALU.mult), a,
                    W("G", t - RV), W("am", t - RV), W("tm", t - RV), T["z1"])
            DVE.put(lambda e: e.scalar_tensor_tensor(tcm[:, r, :], row, col, lc, ALU.is_equal, ALU.mult), W("G", t - 2))
            c = DVE.put(lambda e: e.scalar_tensor_tensor(trm[:, r, :], row, col, gt, ALU.is_equal, ALU.mult))
            T["msk", t] = c
            T["pl", t] = bank_free[0] = DVE.put(lambda e: e.tensor_copy(pl[:, t + 1:t + 2], ps[:, 0, 127:128]), T["z5"])
            DVE.put(lambda e: e.tensor_tensor(fl[:, 0, t:t + 1], col, pl[:, t:t + 1], ALU.is_equal), T["pl", t - 1],
                    T["pl", t])
            T["fl", t] = DVE.put(lambda e: e.tensor_tensor(fl[:, 1, t:t + 1], col, pl[:, t + 1:t + 2], ALU.is_equal))

        def g_kqT(t):
            r = t % 2
            for i in range(4):
                a = tr(ps[:, 3, 128 * i:128 * i + 128], kq[:, r, 128 * i:128 * i + 128], 128, T["kq", t], bankw(3),
                       sig=i == 3)
            T["kqT_p", t] = a
            c = ACTE.put(lambda e: e.activation(qT[:, t % 3, :, :].rearrange("p a n -> p (a n)"), ps[:, 3, 256:512],
                                                ACT.Copy), a, W("p2", t - 3), W("at", t - 3), T["z1"])
            for hb in range(2):
                c = ACTE.put(lambda e, hb=hb: e.activation(
                    ktz[64 * hb:64 * hb + 64, r, hb:4:2, :], v2(ps[64 * hb:64 * hb + 64, 3, 0:256]), ACT.Copy), a,
                    W("at", t - 2), T["z1"])
            T["kqT", t] = bank_free[3] = c

        def g_decay(t):
            r = t % 2
            mm(ps[:, 4, 0:256], tcm[:, r, :], fm[:, r, :], True, True, T["msk", t], T["g8", t], bankw(4))
            a = mm(ps[:, 4, 256:512], mc[:, t % RV, :], fm[:, r, :], True, True, sig=True)
            b = mm(ps[:, 5, 0:256], trm[:, r, :], fm[:, r, :], True, True, bankw(5), sig=True)
            T["G", t] = b
            T["dc", t] = ACTE.put(lambda e: e.activation(dc[:, t % 3, :], ps[:, 4, :], ACT.Exp, scale=0.125), a,
                                  W("o2", t - 3), W("ok", t - 3), W("qg", t - 3), T["z1"])
            c = ACTE.put(lambda e: e.activation(ed[:, r, :], ps[:, 4, 0:256], ACT.Exp, scale=-0.125), W("si", t - 2))
            bank_free[4] = c
            T["si", t] = POOL.put(lambda e: e.tensor_tensor(si[:, t % 3, :], ss[:, r, :], ed[:, r, :], ALU.mult), c,
                                  T["ss", t], W("p1", t - 3), W("siT_p", t - 3))
            c = ACTE.put(lambda e: e.activation(dr[:, r, :], ps[:, 5, 0:256], ACT.Exp, scale=0.125), b, W("h_p", t - 2))
            bank_free[5] = c
            T["srem", t] = DVE.put(lambda e: e.scalar_tensor_tensor(dr[:, r, :], dr[:, r, :], fl[:, 1, t:t + 1],
                                                                    ss[:, r, :], ALU.mult, ALU.mult), c, T["fl", t],
                                   T["ss", t])

        def g_at(t):
            r = t % 2
            for h in range(4):
                a = mm(ps[:, 6, 128 * h:128 * h + 128], ktz[:, r, h, :], qT[:, t % 3, h // 2, :], True, True,
                       T["kqT", t], bankw(6), sig=h == 3)
            T["at", t] = a
            T["am", t] = bank_free[6] = DVE.put(lambda e: e.tensor_tensor(
                am[:, r, :, :], v4(ps[:, 6, :]), mc[:, t % RV, :].unsqueeze(1).to_broadcast([128, 4, 128]), ALU.mult),
                a, T["msk", t], W("p1", t - 2))

        def g_state(t):
            r = t % 2
            for i in range(2):
                mm(ps[:, 5, 128 * i:128 * i + 128], kq[:, r, 128 * i:128 * i + 128], dr[:, r, 128 * i:128 * i + 128],
                   True, True, T["srem", t], T["kq", t], bankw(5))
                a = mm(ps[:, 5, 256 + 128 * i:384 + 128 * i], dr[:, r, 128 * i:128 * i + 128],
                       vv[:, t % RV, 128 * i:128 * i + 128], True, True, T["vv", t], sig=i == 1)
            T["h_p", t] = a
            T["hz", t] = DVE.put(lambda e: e.tensor_tensor(hz[:, t % 4, :, :], v2(ps[:, 5, 0:256]), bd2, ALU.mult), a,
                                 W("p2", t - 3), T["z4"])
            T["hv", t] = bank_free[5] = DVE.put(lambda e: e.tensor_tensor(hv[:, t % 4, :, :], v2(ps[:, 5, 256:512]),
                                                                          bd2, ALU.mult), a, W("ov", t - 3))

        def g_siT(t):
            for i in range(2):
                a = tr(ps[:, 0, 128 * i:128 * i + 128], si[:, t % 3, 128 * i:128 * i + 128], 128, T["si", t],
                       bankw(0), sig=i == 1)
            T["siT_p", t] = a
            for hb in range(2):
                c = ACTE.put(lambda e, hb=hb: e.activation(
                    stz[64 * hb:64 * hb + 64, t % 3, hb:4:2, :], v2(ps[64 * hb:64 * hb + 64, 0, 0:256]), ACT.Copy), a,
                    W("tm_p", t - 3), T["z2"])
            T["stz", t] = bank_free[0] = c

        def g_ok(t):
            r = t % 2
            for h in range(4):
                a = mm(ps[:, 7, 64 * h:64 * h + 64], am[:, r, h, :], si[:, t % 3, 64 * h:64 * h + 64], True, True,
                       T["am", t], T["si", t], bankw(7))
            for i in range(2):
                a = mm(ps[:, 7, 256 + 128 * i:384 + 128 * i], qT[:, t % 3, i, :], hz[:, (t - 1) % 4, i, :], True, True,
                       T["hz", t - 1], sig=i == 1)
            T["p1", t] = T["p2", t] = a
            d, d0 = dc[:, t % 3, 0:256], dc[:, t % 3, 256:512]
            first = fl[:, 0, t:t + 1]
            c = DVE.put(lambda e: e.tensor_tensor(ok[:, r, :], ps[:, 7, 0:256], d, ALU.mult), a, T["dc", t],
                        W("qg", t - 2))
            b = DVE.put(lambda e: e.scalar_tensor_tensor(o2[:, r, :], ps[:, 7, 256:512], first, d0, ALU.mult, ALU.mult),
                        T["fl", t], W("ok", t - 2))
            T["o2", t] = bank_free[7] = b
            c = T["ok", t] = POOL.put(lambda e: e.tensor_tensor(ok[:, r, :], ok[:, r, :], o2[:, r, :], ALU.add), b, c)
            s4 = sm4[:, t % 4, :]
            b = DVE.put(lambda e: e.tensor_reduce(s4[:, 0:4], v4(ok[:, r, :]), axis=X, op=ALU.max), c, W("oo", t - 4))
            c = POOL.put(lambda e: e.tensor_tensor(v4(ok[:, r, :]), v4(ok[:, r, :]),
                                                   s4[:, 0:4].unsqueeze(2).to_broadcast([128, 4, 64]), ALU.subtract),
                         b)
            T["eok", t] = ACTE.put(lambda e: e.activation(ok[:, r, :], ok[:, r, :], ACT.Exp), c)

        def g_qg(t):
            r = t % 2
            d, d0 = dc[:, t % 3, 0:256], dc[:, t % 3, 256:512]
            first = fl[:, 0, t:t + 1]
            s4 = sm4[:, t % 4, :]
            e0 = T["eok", t]
            b = DVE.put(lambda e: e.tensor_reduce(s4[:, 4:8], v4(ok[:, r, :]), axis=X, op=ALU.add), e0)
            T["rz", t] = DVE.put(lambda e: e.reciprocal(s4[:, 4:8], s4[:, 4:8]), b)
            b = POOL.put(lambda e: e.tensor_tensor(qg[:, r, 0:256], ok[:, r, :], d, ALU.mult), e0, W("qgT_p", t - 2))
            c = DVE.put(lambda e: e.scalar_tensor_tensor(qg[:, r, 256:512], ok[:, r, :], first, d0, ALU.mult, ALU.mult),
                        W("qgT_p", t - 2))
            T["qg", t] = c
            for i in range(4):
                a = tr(ps[:, 3, 128 * i:128 * i + 128], qg[:, r, 128 * i:128 * i + 128], 128, b, c, bankw(3),
                       sig=i == 3)
            T["qgT_p", t] = a
            T["qgT", t] = bank_free[3] = ACTE.put(lambda e: e.activation(qgT[:, r, :], ps[:, 3, :], ACT.Copy), a,
                                                  W("ov", t - 2), W("tm_p", t - 2))

        def g_tm(t):
            r = t % 2
            for h in range(4):
                a = mm(ps[:, 6, 128 * h:128 * h + 128], stz[:, t % 3, h, :], qgT[:, r, 128 * (h // 2):128 * (h // 2) + 128],
                       True, True, T["stz", t], T["qgT", t], bankw(6), sig=h == 3)
            T["tm_p", t] = a
            T["tm", t] = bank_free[6] = DVE.put(lambda e: e.tensor_tensor(
                tm[:, r, :, :], v4(ps[:, 6, :]), mc[:, t % RV, :].unsqueeze(1).to_broadcast([128, 4, 128]), ALU.mult),
                a, W("ov", t - 2))

        osem = [dsem("osem0"), dsem("osem1")]

        def g_ov(t):
            r = t % 2
            for i in range(2):
                mm(ps[:, 7, 128 * i:128 * i + 128], qgT[:, r, 256 + 128 * i:384 + 128 * i], hv[:, (t - 1) % 4, i, :],
                   True, False, T["hv", t - 1], T["tm", t], bankw(7))
                for h in (2 * i, 2 * i + 1):
                    a = mm(ps[:, 7, 64 * h:64 * h + 64], tm[:, r, h, :], vv[:, t % RV, 64 * h:64 * h + 64], False,
                           h == 2 * i + 1, sig=h == 3)
            T["ov", t] = a
            c = DVE.put(lambda e: e.tensor_tensor(v4(oo[:, r, :]), v4(ps[:, 7, 0:256]),
                                                  sm4[:, t % 4, 4:8].unsqueeze(2).to_broadcast([128, 4, 64]), ALU.mult),
                        a, T["rz", t], W("od", t - 2))
            T["oo", t] = bank_free[7] = c
            T["od", t] = SP.dma(lambda e: e.dma_start(o_d[128 * t:128 * t + 128, :], oo[:, r, :]), osem[r], c)

        regs = []
        for t in range(RX):
            g_load(t)
        early = [g_x, g_proj, g_mask, g_kqT, g_decay]
        mid = [g_at, g_state, g_siT, g_ok]
        late = [g_qg, g_tm, g_ov]
        for n in range(NT + 2):
            a_, b_, c_ = n, n - 1, n - 2
            plan = [(g_x, a_), (g_at, b_), (g_qg, c_), (g_proj, a_), (g_state, b_), (g_siT, b_), (g_tm, c_),
                    (g_mask, a_), (g_ok, b_), (g_ov, c_), (g_kqT, a_), (g_decay, a_)]
            for f, t in plan:
                if 0 <= t < NT:
                    f(t)

        fin = G("fin", [S, 4, 2, 256])
        fT = G("fT", [128, 2, 2, S])
        fr = G("fr", [S, NB, 4])
        gsem = [dsem(f"gsem{i}") for i in range(4)]
        d_out = dsem("d_out")
        fin_end = []

        def f_gather(b):
            for k in range(2):
                T["ga", b] = POOL.dma(lambda e, k=k: e.indirect_dma_start(
                    out=fin[:, b % 4, k, :], out_offset=None, in_=o_d.ap(),
                    in_offset=bass.IndirectOffsetOnAxis(ap=idx[:, k, b:b + 1], axis=0)), gsem[b % 4],
                    T["od", NT - 1], T["od", NT - 2], W("fs", b - 4))

        def f_sum(b):
            f0, f1 = fin[:, b % 4, 0, :], fin[:, b % 4, 1, :]
            a = DVE.put(lambda e: e.tensor_scalar(f0, f0, rwt[:, 0, b:b + 1], None, ALU.mult), T["ga", b])
            a = DVE.put(lambda e: e.scalar_tensor_tensor(f0, f1, rwt[:, 1, b:b + 1], f0, ALU.mult, ALU.add), a)
            a2 = ACTE.put(lambda e: e.activation(f1, f0, ACT.Square, accum_out=fr[:, b, 0:1]), a)
            a2 = POOL.put(lambda e: e.tensor_scalar(fr[:, b, 1:2], fr[:, b, 0:1], 1.0 / D, 1e-5, ALU.mult, ALU.add), a2)
            a2 = POOL.put(lambda e: e.tensor_tensor(fr[:, b, 2:3], fr[:, b, 1:2], epow[:, :], ALU.pow), a2)
            T["fs0", b] = (a, a2)

        def f_norm(b):
            f0 = fin[:, b % 4, 0, :]
            a = DVE.put(lambda e: e.scalar_tensor_tensor(f0, f0, fr[:, b, 2:3], rw_sb[:, 4, :], ALU.mult, ALU.mult),
                        *T["fs0", b])
            k0 = b % 2
            for i in range(2):
                a1 = tr(ps[:, k0, S * i:S * i + S], f0[:, 128 * i:128 * i + 128], S, a, bankw(k0), sig=i == 1)
            T["fs", b] = a1
            T["fT", b] = bank_free[k0] = ACTE.put(lambda e: e.activation(
                fT[:, b % 2, :, :].rearrange("p t n -> p (t n)"), ps[:, k0, 0:2 * S], ACT.Copy), a1, W("fo2", b - 2))

        def f_out(b):
            k0 = 2 + b % 2
            for i in range(2):
                a = mm(ps[0:S, k0, 0:256], fT[:, b % 2, i, :], wom[:, i, :], i == 0, i == 1, T["fT", b], T["wom"],
                       bankw(k0), sig=i == 1)
            T["fo2", b] = a
            c = bank_free[k0] = DVE.put(lambda e: e.tensor_tensor(x2[:, b, :], x2[:, b, :], ps[0:S, k0, 0:256],
                                                                  ALU.add), a)
            T["done"] = SP.dma(lambda e: e.dma_start(out[b], x2[:, b, :]), d_out, c)

        for n in range(NB + 3):
            for f, b in ((f_gather, n), (f_sum, n - 1), (f_norm, n - 2), (f_out, n - 3)):
                if 0 <= b < NB:
                    f(b)
        SP.put(lambda e: e.nop(), T["done"], T["zero"], T["xs_all"], T["od", NT - 1], T["od", NT - 2], sig=False)

        blk = root.enter_context(nc.Block())

        @blk.sync
        def _(e):
            SP.play(e)

        @blk.tensor
        def _(e):
            regs.append(e.alloc_register("expert"))
            PE.play(e)

        @blk.vector
        def _(e):
            DVE.play(e)

        @blk.scalar
        def _(e):
            ACTE.play(e)

        @blk.gpsimd
        def _(e):
            POOL.play(e)


def constants():
    import numpy as np
    c = np.zeros((128, C_N), np.float32)
    j, i = np.arange(128)[:, None], np.arange(128)[None, :]
    c[:, C_ID:C_ID + 128] = j == i
    c[:, C_LE:C_LE + 128] = j <= i
    c[:, C_LC:C_LC + 128] = (j <= i) * 1.0 - (j <= 63) * 1.0
    c[:, C_GT:C_GT + 128] = j > i
    c[:, C_LT:C_LT + 128] = j < i
    c[:, C_BD:C_BD + 128] = j // 16 == i // 16
    c[:, C_BD2:C_BD2 + 128] = j // 64 == i // 64
    c[:, C_HM:C_HM + 8] = j // 16 == np.arange(8)[None, :]
    c[:, C_PR:C_PR + 64] = 8 - np.arange(64)[None, :] % 8
    c[:, C_SL:C_SL + 21] = 128 * np.arange(21)[None, :] + j
    c[:, C_TH:C_TH + 7] = 128 * np.arange(7)[None, :]
    c[:, C_CB:C_CB + 112] = np.where(i[:, 0:112] > j, -1e30, 0.0)
    return c


def kernel(**inputs):
    import numpy as np
    import concourse.bacc as bacc
    from concourse.bass_utils import run_bass_kernel_spmd

    g = {k: np.asarray(v) for k, v in inputs.items()}
    c = np.ascontiguousarray
    ffn = np.concatenate([g["L0_ffn_Wk"].transpose(0, 2, 1), g["L0_ffn_Wv"].transpose(0, 2, 1),
                          g["L0_ffn_Wf"].transpose(0, 2, 1)], axis=2)
    arrays = {
        "x": g["x"], "ctx": g["ctx_1024"], "ctxT": g["ctx_1024"].transpose(0, 2, 1), "mask": g["mask_Bx1xSxS2_ik1"],
        "wself": np.stack([g["L0_attn_Wq"], g["L0_attn_Wk"], g["L0_attn_Wv"], g["L0_attn_Wo"]]),
        "bself": np.stack([g["L0_attn_bq"][0:128], g["L0_attn_bq"][128:], g["L0_attn_bk"][0:128],
                           g["L0_attn_bk"][128:]], axis=1),
        "wxq": np.tile(g["L0_xattn_Wq"], (1, 8)), "wxk": np.tile(g["L0_xattn_Wk"], (1, 8)),
        "wxv": np.tile(g["L0_xattn_Wv"], (8, 8)), "wxo": g["L0_xattn_Wo"].T,
        "rows": np.concatenate([g["L0_attn_bv"], g["L0_attn_bo"], g["L0_xattn_bo"], g["L0_ffn_norm_w"],
                                g["L0_ffn_gnorm_w"]]),
        "wg": g["L0_ffn_Wg"].T, "wmoe": ffn, "wq_moe": g["L0_ffn_Wq"].T, "wo_moe": g["L0_ffn_Wo"].T,
        "consts": constants(),
    }
    arrays = {"in_" + k: c(v) for k, v in arrays.items()}
    nc = bacc.Bacc("TRN2", target_bir_lowering=False, num_devices=1)
    args = [nc.dram_tensor(k, a.shape, mybir.dt.from_np(a.dtype), kind="ExternalInput").ap() for k, a in arrays.items()]
    args.append(nc.dram_tensor("out0", (NB, S, D), mybir.dt.float32, kind="ExternalOutput").ap())
    decoder_kernel(nc, *args)
    r = run_bass_kernel_spmd(nc, [arrays], core_ids=[0])
    return r.results[0]["out0"]
```

```python
import concourse.bass as bass
from concourse import mybir
from contextlib import ExitStack

NB, S, D, NK = 8, 112, 256, 375
KC, NC3 = 125, 3
NE, NT = 8, 21
NSLOT = NT * 128
WC = 2 * 768
C_ID, C_LE, C_LC, C_GT, C_LT, C_BD, C_BD2, C_HM, C_PR, C_SL, C_TH, C_CB = (
    0, 128, 256, 384, 512, 640, 768, 896, 904, 968, 989, 996)
C_N = C_CB + 112


class Queue:

    def __init__(self, sem):
        self.sem, self.n, self.items = sem, 0, []

    def put(self, fn, *waits, sig=True):
        self.items.append((fn, [w for w in waits if w is not None], sig))
        if sig:
            self.n += 1
            return (self.sem, self.n)
        return None

    def dma(self, fn, sem, *waits):
        sem[1] += 16
        self.items.append((fn, [w for w in waits if w is not None], sem[0]))
        return (sem[0], sem[1])

    def play(self, eng):
        seen = {}
        for fn, waits, sig in self.items:
            for s, v in waits:
                if seen.get(id(s), 0) < v:
                    eng.wait_ge(s, v)
                    seen[id(s)] = v
            ins = fn(eng)
            if sig is True:
                ins.then_inc(self.sem, 1)
            elif sig is not False:
                ins.then_inc(sig, 16)


def decoder_kernel(nc, x, ctx, ctxT, mask, wself, wos_d, bself, wxq, wxk, wxv, wxo, rows, wg, wmoe, wq_moe, wo_moe,
                   consts, out):
    f32, bf16, i32 = mybir.dt.float32, mybir.dt.bfloat16, mybir.dt.int32
    ALU, ACT, AX = mybir.AluOpType, mybir.ActivationFunctionType, mybir.AxisListType
    X = AX.X
    root = ExitStack()
    with root:
        def sbuf(stack, name, shape, dt=f32):
            return stack.enter_context(nc.sbuf_tensor(name, shape, dt))

        def semaphore(name):
            return root.enter_context(nc.semaphore(name))

        PE, DVE, ACTE, POOL, SP = (Queue(semaphore(n)) for n in ("q_pe", "q_dve", "q_act", "q_pool", "q_sp"))
        dsem = lambda name: [semaphore(name), 0]
        T = {}

        def W(*key):
            return T.get(key)

        ps = root.enter_context(nc.psum_tensor("ps", [128, 8, 512], f32))
        bank_free = {7: None}

        cst = sbuf(root, "cst", [128, C_N])
        xbo = sbuf(root, "xbo", [S, NB, D])
        y = sbuf(root, "y", [S, NB, D])
        wm = sbuf(root, "wm", [128, NE * WC])
        wqm = sbuf(root, "wqm", [128, 2, 256])
        wom = sbuf(root, "wom", [128, 2, 256])
        rw_sb = sbuf(root, "rw_sb", [S, 5, 256])
        lg = sbuf(root, "lg", [S, NB, NE])
        st = sbuf(root, "st", [S, NB, 3, 12])
        epow = sbuf(root, "epow", [S, 1])
        zer = sbuf(root, "zer", [128, 256])
        rwt_ = sbuf(root, "rwt", [S, 2, NB])
        idx_ = sbuf(root, "idx", [S, 2, NB], i32)
        segc_ = sbuf(root, "segc", [128, NT])
        et1_ = sbuf(root, "et1", [1, NT])
        eti_ = sbuf(root, "eti", [1, NT], i32)
        one_ = sbuf(root, "one_", [S, 128])
        one64_128 = one_[:, :]
        ident = cst[:, C_ID:C_ID + 128]
        x2 = xbo
        xs_d = nc.dram_tensor("xs_d", [NSLOT, 256], f32)
        o_d = nc.dram_tensor("o_d", [NSLOT, 256], f32)

        att = ExitStack()
        ws = sbuf(att, "ws", [128, 3, 2, 256])
        wos = sbuf(att, "wos", [128, 4, 256])
        bqk = sbuf(att, "bqk", [128, 4])
        wxq_s = sbuf(att, "wxq_s", [16, 128])
        wxk_s = sbuf(att, "wxk_s", [16, 128])
        bdv = sbuf(att, "bdv", [128, 128])
        wxo_s = sbuf(att, "wxo_s", [128, 4, 256])
        wg_s = sbuf(att, "wg_s", [128, 2, NE])
        bdq = sbuf(att, "bdq", [128, 128])
        fo = sbuf(att, "fo", [128, 4, 256])
        idb = sbuf(att, "idb", [S, S], bf16)
        cmb = sbuf(att, "cmb", [S, 4, S], bf16)
        hmq = sbuf(att, "hmq", [128, 8, S])
        hms = sbuf(att, "hms", [128, 8, S])
        mki = sbuf(att, "mki", [S, 2, NK], i32)
        mkb = sbuf(att, "mkb", [S, NB, NK], bf16)
        cx = sbuf(att, "cx", [KC, 3, NC3, D + 16])
        cxT = sbuf(att, "cxT", [128, 3, 2, NK])
        xn = sbuf(att, "xn", [S, 2, D])
        xnT = sbuf(att, "xnT", [128, 2, 2, S])
        qk = sbuf(att, "qk", [128, 2, 4, S])
        va = sbuf(att, "va", [S, 2, D + 16])
        qz = sbuf(att, "qz", [128, 4, 2, 8, S])
        qx = sbuf(att, "qx", [128, 2, S])
        PR = 4
        pr = sbuf(att, "pr", [S, PR, 4 * S])
        pt = sbuf(att, "pt", [KC, PR, 4, S])
        mx = sbuf(att, "mx", [S, NB, 2, 2, 16])
        sm = sbuf(att, "sm", [S, 2, 16])
        smx = sbuf(att, "smx", [S, 2, 16, 32])
        rT = sbuf(att, "rT", [128, 2, 4, S])
        onT = sbuf(att, "onT", [128, 2, 4, S])
        yT = sbuf(att, "yT", [128, 2, 2, S])
        sq = sbuf(att, "sq", [S, D])
        x1 = sbuf(att, "x1", [S, 2, D])

        def load(name, dst, src, q=SP, *waits):
            T[name] = q.dma(lambda e: e.dma_start(dst, src), dsem("l_" + name), *waits)

        xr = x.rearrange("b s d -> s b d")
        load("x0", xbo[:, 0:2, :], xr[:, 0:2, :])
        load("cst", cst[:, :], consts)
        load("ws", ws[:, :, :, :], wself.rearrange("w (t p) n -> p w t n", p=128))
        load("bqk", bqk[:, :], bself)
        load("rows", rw_sb[:, :, :].rearrange("p a n -> p (a n)"), rows.partition_broadcast(S))
        d_mk = [dsem("d_mk0"), dsem("d_mk1")]
        d_cx = [dsem(f"d_cx{i}") for i in range(3)]
        d_ct = [dsem(f"d_ct{i}") for i in range(3)]
        cxr = ctx.rearrange("b (c p) d -> b p c d", p=KC)

        def load_mask(b):
            T["mki", b] = SP.dma(lambda e: e.dma_start(mki[:, b % 2, :], mask[b, 0, :, :]), d_mk[b % 2], W("mkb", b - 2))

        def load_ctx(b):
            T["cx", b] = SP.dma(lambda e: e.dma_start(cx[:, b % 3, :, 0:D], cxr[b]), d_cx[b % 3], W("pv", "c", b - 3))
            T["cxT", b] = SP.dma(lambda e: e.dma_start(cxT[:, b % 3, :, :], ctxT[b].rearrange("(t p) k -> p t k", p=128)),
                                 d_ct[b % 3], W("st", "c", b - 3))

        load_mask(0)
        load_ctx(0)
        load("wxq", wxq_s[:, :], wxq)
        load("wxk", wxk_s[:, :], wxk)
        load("wxv", bdv[:, :], wxv)
        load("wxo", wxo_s[:, :, :], wxo.rearrange("g p n -> p g n"))
        load("wos", wos[:, :, :], wos_d.rearrange("g p n -> p g n"))
        load("wg", wg_s[:, :, :], wg.rearrange("(t p) n -> p t n", p=128))
        load("x", xbo[:, 2:NB, :], xr[:, 2:NB, :])
        load_mask(1)
        load_ctx(1)
        load_ctx(2)
        load("wqm", wqm[:, :, :], wq_moe.rearrange("(t p) n -> p t n", p=128))
        load("wom", wom[:, :, :], wo_moe.rearrange("(t p) n -> p t n", p=128))
        for e8 in range(NE):
            load(f"wm{e8}", wm[:, e8 * WC:(e8 + 1) * WC].rearrange("p (t n) -> p t n", t=2),
                 wmoe[e8].rearrange("(t p) n -> p t n", p=128))

        ACTE.put(lambda e: e.preload_act_table_set("natural_log_exp_and_others"), sig=False)
        T["zer"] = POOL.put(lambda e: e.memset(zer[:, :], 0.0))
        T["epow"] = POOL.put(lambda e: e.memset(epow[:, :], -0.5))
        T["ones"] = POOL.put(lambda e: e.memset(one_[:, :], 1.0))
        T["vpad"] = POOL.put(lambda e: e.memset(va[:, :, D:D + 16], 0.0))
        T["cpad"] = POOL.put(lambda e: e.memset(cx[:, :, :, D:D + 16], 0.0))
        T["hmq"] = DVE.put(lambda e: e.tensor_copy(
            hmq[:, :, :], cst[:, C_HM:C_HM + 8].unsqueeze(2).to_broadcast([128, 8, S])), T["cst"])
        T["hms"] = DVE.put(lambda e: e.tensor_scalar(hms[:, :, :], hmq[:, :, :], 0.25, None, ALU.mult), T["hmq"])
        T["idb"] = DVE.put(lambda e: e.tensor_copy(idb[:, :], cst[0:S, C_ID:C_ID + S]), T["cst"])
        T["cmb"] = DVE.put(lambda e: e.tensor_copy(
            cmb[:, :, :], cst[0:S, C_CB:C_CB + S].unsqueeze(1).to_broadcast([S, 4, S])))
        zsem = dsem("zsem")
        for i in range(NT):
            T["zero"] = SP.dma(lambda e, i=i: e.dma_start(xs_d[128 * i:128 * i + 128, :], zer[:, :]), zsem, T["zer"])

        def mm(o, l, r, start, stop, *waits, sig=False):
            return PE.put(lambda e: e.matmul(o, l, r, start=start, stop=stop), *waits, sig=sig)

        def tr(o, i, n, *waits, sig=False):
            return PE.put(lambda e: e.transpose(o, i, ident[0:n, 0:n]), *waits, sig=sig)

        def ln_stats(src, b, j, *waits):
            v = st[:, b, j, :]
            a = DVE.put(lambda e: e.bn_stats(v[:, 0:6], src), *waits)
            a = DVE.put(lambda e: e.bn_aggr(v[:, 6:8], v[:, 0:6]), a)
            a = POOL.put(lambda e: e.tensor_scalar(v[:, 8:9], v[:, 7:8], 1e-5, None, ALU.add), a, T["epow"])
            return POOL.put(lambda e: e.tensor_tensor(v[:, 9:10], v[:, 8:9], epow[:, :], ALU.pow), a)

        def ln_apply(dst, src, b, j, *waits):
            v = st[:, b, j, :]
            return DVE.put(lambda e: e.tensor_scalar(dst, src, v[:, 6:7], v[:, 9:10], ALU.subtract, ALU.mult), *waits)

        def xn_stats(kind, b):
            src = xbo[:, b, :] if kind == "s" else x1[:, b % 2, :]
            T["xn_stats", kind, b] = ln_stats(src, b, 0 if kind == "s" else 1, (T["x0"] if b < 2 else T["x"]) if kind == "s" else T["x1", b])

        def make_xn(kind, b):
            j = 0 if kind == "s" else 1
            src = xbo[:, b, :] if kind == "s" else x1[:, b % 2, :]
            T["xn", kind, b] = ln_apply(xn[:, j, :], src, b, j, T["xn_stats", kind, b],
                                        W("xnT" + kind + "_tr", b - 1))
            if kind == "s":
                T["xbo", b] = POOL.put(lambda e: e.tensor_tensor(xbo[:, b, :], xbo[:, b, :], rw_sb[:, 1, :], ALU.add),
                                       T["xn", kind, b], T["rows"])
            else:
                T["x1b", b] = POOL.put(lambda e: e.tensor_tensor(x2[:, b, :], x1[:, b % 2, :], rw_sb[:, 2, :], ALU.add),
                                       T["x1", b], T["xn", "c", b])

        def transpose2(key, src, dst, b, *waits, free=None):
            for t in range(2):
                a = tr(ps[:, 7, S * t:S * t + S], src[:, 128 * t:128 * t + 128], S, bank_free[7], T["cst"], *waits,
                       sig=t == 1)
            T[key + "_tr", b] = a
            r = ACTE.put(lambda e: e.activation(dst.rearrange("p t n -> p (t n)"), ps[:, 7, 0:2 * S], ACT.Copy), a,
                         free)
            bank_free[7] = r
            return r

        def make_xnT(kind, b):
            j = 0 if kind == "s" else 1
            T["xnT", kind, b] = transpose2("xnT" + kind, xn[:, j, :], xnT[:, j, :, :], b,
                                           T["xn", kind, b], free=W("xnT_used", kind, b - 1))

        def self_qk(b):
            for w in range(2):
                for m in range(2):
                    for t in range(2):
                        a = mm(ps[:, 7, (2 * w + m) * S:(2 * w + m + 1) * S], ws[:, w, t, 128 * m:128 * m + 128],
                               xnT[:, 0, t, :], t == 0, t == 1, bank_free[7], T["xnT", "s", b], T["ws"],
                               sig=(w, m, t) == (1, 1, 1))
            r = DVE.put(lambda e: e.tensor_tensor(qk[:, b % 2, :, :], ps[:, 7, 0:4 * S].rearrange("p (a n) -> p a n", a=4),
                                                  bqk[:, :].unsqueeze(2).to_broadcast([128, 4, S]), ALU.add),
                        a, T["bqk"], W("st", "s", b - 2), W("qz", "s", b - 2, 0), W("qz", "s", b - 2, 1))
            T["qk", b] = bank_free[7] = r

        def self_v(b):
            for t in range(2):
                a = mm(ps[0:S, 7, 0:256], xnT[:, 0, t, :], ws[:, 2, t, :], t == 0, t == 1, bank_free[7],
                       T["xnT", "s", b], sig=t == 1)
            T["xnT_used", "s", b] = a
            r = DVE.put(lambda e: e.tensor_tensor(
                va[:, b % 2, 0:D], ps[0:S, 7, 0:256], rw_sb[:, 0, :], ALU.add), a, T["rows"], T["vpad"],
                W("pv", "s", b - 2))
            T["va", b] = bank_free[7] = r

        def make_qz(kind, b):
            k = (0 if kind == "s" else 2) + b % 2
            hm = hms if kind == "s" else hmq
            for t in range(2):
                src = qk[:, b % 2, t, :] if kind == "s" else qx[:, t, :]
                q = DVE if b < 2 and t == 0 else POOL
                T["qz", kind, b, t] = q.put(lambda e, src=src, t=t: e.tensor_tensor(
                    qz[:, k, t, :, :], src.unsqueeze(1).to_broadcast([128, 8, S]), hm[:, :, :], ALU.mult),
                    T["qk" if kind == "s" else "qx", b], T["hms"], W("st", kind, b - 2))

        def cross_q(b):
            for t in range(2):
                a = mm(ps[:, 7, S * t:S * t + S], bdq[:, :], xnT[:, 1, t, :], True, True, bank_free[7],
                       T["xnT", "c", b], T["bdq"], sig=t == 1)
            T["xnT_used", "c", b] = a
            r = ACTE.put(lambda e: e.activation(qx[:, :, :].rearrange("p t n -> p (t n)"), ps[:, 7, 0:2 * S], ACT.Copy),
                         a, W("qz", "c", b - 1, 0), W("qz", "c", b - 1, 1))
            T["qx", b] = bank_free[7] = r

        def mask_bias(b):
            T["mkb", b] = DVE.put(lambda e: e.tensor_scalar(mkb[:, b, :], mki[:, b % 2, :], 0.0, 1e20,
                                                            ALU.is_equal, ALU.mult), T["mki", b])
            if b + 2 < NB:
                load_mask(b + 2)

        def inverse_sums(kind, b):
            k = 0 if kind == "s" else 1
            a = DVE.put(lambda e: e.reciprocal(sm[:, k, :], mx[:, b, k, 1, :]), T["P", kind, b])
            T["smx", kind, b] = DVE.put(lambda e: e.tensor_copy(
                smx[:, k, :, :], sm[:, k, :].unsqueeze(2).to_broadcast([S, 16, 32])), a, W("rT_p", kind, b - 1))

        def spread_sums(kind, b):
            k = 0 if kind == "s" else 1
            for g in range(4):
                c = tr(ps[:, 7, S * g:S * g + S], smx[:, k, 4 * g:4 * g + 4, :].rearrange("p a n -> p (a n)"), S,
                       T["smx", kind, b], bank_free[7], sig=g == 3)
            T["rT_p", kind, b] = c
            T["rT", kind, b] = bank_free[7] = ACTE.put(lambda e: e.activation(
                rT[:, k, :, :].rearrange("p t n -> p (t n)"), ps[:, 7, 0:4 * S], ACT.Copy), c, W("onT", kind, b - 1))

        def normed(kind, b):
            k = 0 if kind == "s" else 1
            r = DVE.put(lambda e: e.tensor_tensor(
                onT[:, k, :, :].rearrange("p t n -> p (t n)"), ps[:, 5 + k, 0:4 * S],
                rT[:, k, :, :].rearrange("p t n -> p (t n)"), ALU.mult), T["rT", kind, b], T["pv", kind, b],
                W("op", kind, b - 1))
            T["onT", kind, b] = bank_free[5 + k] = r

        def out_proj(kind, b):
            k = 0 if kind == "s" else 1
            for g in range(4):
                w = wos[:, g, :] if kind == "s" else fo[:, g, :]
                a = mm(ps[0:S, 7, 0:256], onT[:, k, g, :], w, g == 0, g == 3, bank_free[7], T["onT", kind, b],
                       T["fo"], T["wos"], sig=g == 3)
            T["op", kind, b] = a
            if kind == "s":
                r = DVE.put(lambda e: e.tensor_tensor(x1[:, b % 2, :], ps[0:S, 7, 0:256], xbo[:, b, :], ALU.add), a,
                            T["xbo", b], W("x1b", b - 2))
                T["x1", b] = bank_free[7] = r
            else:
                T["x2", b] = bank_free[7] = DVE.put(lambda e: e.tensor_tensor(
                    x2[:, b, :], ps[0:S, 7, 0:256], x2[:, b, :], ALU.add), a, T["x1b", b])

        def ffn_stats(b):
            T["ffn_stats", b] = ln_stats(x2[:, b, :], b, 2, T["x2", b])

        def ffn_norm1(b):
            T["xh", b] = ln_apply(y[:, b, :], x2[:, b, :], b, 2, T["ffn_stats", b])
            v = st[:, b, 2, :]
            a = ACTE.put(lambda e: e.activation(sq[:, :], y[:, b, :], ACT.Square, accum_out=v[:, 10:11]), T["xh", b],
                         W("sq", b - 1))
            T["sq", b] = a
            a = POOL.put(lambda e: e.tensor_scalar(v[:, 8:9], v[:, 10:11], 1.0 / D, 1e-5, ALU.mult, ALU.add), a)
            T["rr", b] = POOL.put(lambda e: e.tensor_tensor(v[:, 11:12], v[:, 8:9], epow[:, :], ALU.pow), a)

        def ffn_norm2(b):
            v = st[:, b, 2, :]
            T["y", b] = DVE.put(lambda e: e.scalar_tensor_tensor(y[:, b, :], y[:, b, :], v[:, 11:12], rw_sb[:, 3, :],
                                                                 ALU.mult, ALU.mult), T["rr", b], T["xh", b])

        def ffn_yT(b):
            T["yT", b] = transpose2("yT", y[:, b, :], yT[:, b % 2, :, :], b, T["y", b], free=W("yT_used", b - 2))

        def ffn_logits(b):
            for t in range(2):
                a = mm(ps[0:S, 7, 0:NE], yT[:, b % 2, t, :], wg_s[:, t, :], t == 0, t == 1, bank_free[7], T["yT", b],
                       T["wg"], sig=t == 1)
            T["yT_used", b] = a
            T["lg", b] = bank_free[7] = DVE.put(lambda e: e.tensor_copy(lg[:, b, :], ps[0:S, 7, 0:NE]), a)

        units = []
        EB, PB = 3, 2

        def unit_scores(n):
            kind, b, g = units[n]
            bk = n % EB
            if kind == "s":
                mm(ps[0:S, bk, 0:4 * S], idb[:, :], cmb[:, :, :].rearrange("p a n -> p (a n)"), True, False,
                   bank_free.get(bk), T["idb"], T["cmb"])
                for i in range(4):
                    h = 4 * g + i
                    a = mm(ps[0:S, bk, S * i:S * i + S], qz[:, b % 2, h // 8, h % 8, :], qk[:, b % 2, 2 + h // 8, :],
                           False, i == 3, T["qz", kind, b, h // 8], T["qk", b], sig=i == 3)
            else:
                a = mm(ps[0:S, bk, 0:NK], qz[:, 2 + b % 2, g // 8, g % 8, :], cxT[:, b % 3, g // 8, :],
                       True, True, T["qz", kind, b, g // 8], T["cxT", b], bank_free.get(bk), sig=True)
            T["E", n] = a
            T["st", kind, b] = a

        def unit_soft(n):
            kind, b, g = units[n]
            bk, r = n % EB, n % PR
            k, nh, w = (0, 4, S) if kind == "s" else (1, 1, NK)
            if kind == "c":
                a = DVE.put(lambda e: e.tensor_tensor_reduce(
                    pr[:, r, 0:NK], ps[0:S, bk, 0:NK], mkb[:, b, :], 1.0, 3e38, ALU.add, ALU.min,
                    mx[:, b, k, 0, g:g + 1]), T["E", n], T["mkb", b], W("T", n - PR))
                bank_free[bk] = a
                T["P", kind, b] = T["P", n] = ACTE.put(lambda e: e.activation(
                    pr[:, r, 0:NK], pr[:, r, 0:NK], ACT.Exp, bias=mx[:, b, k, 0, g:g + 1], scale=-1.0,
                    accum_out=mx[:, b, k, 1, g:g + 1]), a)
                return
            src = ps[0:S, bk, 0:nh * w].rearrange("p (h n) -> p h n", h=nh)
            m4 = mx[:, b, k, 0, nh * g:nh * g + nh]
            a = DVE.put(lambda e: e.tensor_reduce(m4, src, axis=X, op=ALU.max, negate=True), T["E", n])
            for i in range(nh):
                h = nh * g + i
                T["P", n] = ACTE.put(lambda e, i=i, h=h: e.activation(
                    pr[:, r, w * i:w * i + w], ps[0:S, bk, w * i:w * i + w], ACT.Exp, bias=mx[:, b, k, 0, h:h + 1],
                    accum_out=mx[:, b, k, 1, h:h + 1]), a, W("T", n - PR))
            bank_free[bk] = T["P", kind, b] = T["P", n]

        def unit_transpose(n):
            kind, b, g = units[n]
            r, bk = n % PR, 3 + n % PB
            m, w = (4, S) if kind == "s" else (NC3, KC)
            for i in range(m):
                a = tr(ps[0:w, bk, S * i:S * i + S], pr[:, r, w * i:w * i + w], S, T["P", n], bank_free.get(bk),
                       sig=i == m - 1)
            T["T", n] = a
            T["pt", n] = bank_free[bk] = DVE.put(lambda e: e.tensor_copy(
                pt[0:w, r, 0:m, :].rearrange("p a n -> p (a n)"), ps[0:w, bk, 0:m * S]), a, W("PV", n - PR))

        def unit_pv(n):
            kind, b, g = units[n]
            r = n % PR
            last = g == (3 if kind == "s" else 15)
            if last:
                spread_sums(kind, b)
            if kind == "s":
                for i in range(4):
                    h = 4 * g + i
                    a = mm(ps[32 * i:32 * i + 32, 5, S * g:S * g + S], va[:, b % 2, 16 * h:16 * h + 32],
                           pt[0:S, r, i, :], True, True, T["pt", n], T["va", b], bank_free.get(5), sig=i == 3)
            else:
                i, gg = g % 4, g // 4
                for c in range(NC3):
                    a = mm(ps[32 * i:32 * i + 32, 6, S * gg:S * gg + S], cx[:, b % 3, c, 16 * g:16 * g + 32],
                           pt[:, r, c, :], c == 0, c == NC3 - 1, T["pt", n], T["cx", b], T["cpad"],
                           bank_free.get(6), sig=c == NC3 - 1)
            T["PV", n] = a
            T["pv", kind, b] = a
            if last:
                normed(kind, b)
                if kind == "c" and b + 3 < NB:
                    load_ctx(b + 3)

        def prologue(b):
            return [lambda: xn_stats("s", b), lambda: make_xn("s", b), lambda: make_xnT("s", b), lambda: self_qk(b),
                    lambda: (make_qz("s", b), self_v(b))]

        def middle(b):
            return [lambda: (out_proj("s", b), xn_stats("c", b)), lambda: make_xn("c", b),
                    lambda: make_xnT("c", b), lambda: cross_q(b), lambda: make_qz("c", b)]

        def epilogue(b):
            return [lambda: (out_proj("c", b), ffn_stats(b)), lambda: ffn_norm1(b), lambda: ffn_norm2(b),
                    lambda: ffn_yT(b), lambda: ffn_logits(b)]

        def combine():
            T["bdq_p"] = mm(ps[:, 7, 0:128], wxq_s[:, :], wxk_s[:, :], True, True, T["wxq"], T["wxk"], bank_free[7],
                            sig=True)
            T["bdq"] = DVE.put(lambda e: e.scalar_tensor_tensor(bdq[:, :], ps[:, 7, 0:128], -0.0625, cst[:, C_BD:C_BD + 128],
                                                                ALU.mult, ALU.mult), T["bdq_p"])
            for k in range(2):
                for g in (2 * k, 2 * k + 1):
                    a = mm(ps[:, 6 + k, 256 * (g % 2):256 * (g % 2) + 256], bdv[:, :], wxo_s[:, g, :], True, True,
                           T["wxv"], T["wxo"], T["bdq"], sig=True)
                T["fo"] = bank_free[6 + k] = DVE.put(lambda e, k=k: e.tensor_copy(
                    fo[:, 2 * k:2 * k + 2, :].rearrange("p t n -> p (t n)"), ps[:, 6 + k, :]), a)

        xn_stats("s", 0)
        xn_stats("s", 1)
        for f in prologue(0)[1:]:
            f()
        for b in range(2):
            units += [("s", b, g) for g in range(4)]
        for b in range(NB):
            for g in range(16):
                units.append(("c", b, g))
                if g % 4 == 3 and b + 2 < NB:
                    units.append(("s", b + 2, g // 4))
        chains = {"p": prologue(1)[1:] + [combine, lambda: (mask_bias(0), mask_bias(1))], "m": [], "e": []}
        ran = {"p": -9, "m": -9, "e": -9}
        TL, VL = 2, 3

        def side_step(n):
            ready = [k for k in chains if chains[k] and n - ran[k] >= (2 if n > 11 else 1)]
            if ready:
                k = min(ready, key=lambda k: ran[k])
                chains[k].pop(0)()
                ran[k] = n

        def need(k, *key):
            while key not in T:
                chains[k].pop(0)()

        for n in range(len(units) + VL):
            if n < len(units):
                kind, b, g = units[n]
                if kind == "c" and g == 0:
                    need("m", "qz", "c", b, 1)
                    need("p", "mkb", b)
                if kind == "s" and g == 0:
                    need("p", "va", b)
                    if b + 1 < NB and b >= 1:
                        chains["p"] += prologue(b + 1) + [lambda b=b: mask_bias(b + 1)]
                unit_scores(n)
                unit_soft(n)
            if 0 <= n - 1 < len(units):
                k2, b2, g2 = units[n - 1]
                if g2 == (3 if k2 == "s" else 15):
                    inverse_sums(k2, b2)
            if 0 <= n - TL < len(units):
                unit_transpose(n - TL)
            if 0 <= n - VL < len(units):
                unit_pv(n - VL)
                k2, b2, g2 = units[n - VL]
                if g2 == (3 if k2 == "s" else 15):
                    chains["m" if k2 == "s" else "e"] += middle(b2) if k2 == "s" else epilogue(b2)
                    ran["m" if k2 == "s" else "e"] = n
            side_step(n)
        for f in chains["p"] + chains["m"] + chains["e"]:
            f()

        att.close()

        rt = ExitStack()
        R = lambda name, shape, dt=f32: sbuf(rt, name, shape, dt)
        pb = R("pb", [S, NB, NE])
        pc = R("pc", [S, NB, NE])
        m1 = R("m1", [S, NB, NE])
        m2 = R("m2", [S, NB, NE])
        mb = R("mb", [S, NB, NE])
        rd = R("rd", [S, 8, NB])
        cn = R("cn", [128, NB, NE])
        sc = R("sc", [128, NE, NB])
        stt = R("stt", [128, NB, NE])
        e8 = R("e8", [128, 6, NE])
        th = R("th", [128, NE, 7])
        one64 = R("one64", [128, 64])
        seg3 = R("seg3", [128, NT, 64])
        etf = R("etf", [1, NT, NE])
        T["one64"] = POOL.put(lambda e: e.memset(one64[:, :], 1.0))
        rwt, idx, segc, eti, et1 = rwt_, idx_, segc_, eti_, et1_

        def seq(fn, *waits):
            return DVE.put(fn, (DVE.sem, DVE.n), *waits)

        bc8 = lambda a: a.unsqueeze(2).to_broadcast([S, NB, NE])
        lgf = lg[:, :, :]
        seq(lambda e: e.tensor_reduce(rd[:, 0, :], lgf, axis=X, op=ALU.max), T["lg", NB - 1])
        a = seq(lambda e: e.tensor_tensor(pb[:, :, :], lgf, bc8(rd[:, 0, :]), ALU.subtract))
        a = ACTE.put(lambda e: e.activation(pb[:, :, :], pb[:, :, :], ACT.Exp), a)
        seq(lambda e: e.tensor_reduce(rd[:, 1, :], pb[:, :, :], axis=X, op=ALU.add), a)
        seq(lambda e: e.reciprocal(rd[:, 2, :], rd[:, 1, :]))
        seq(lambda e: e.tensor_tensor(pb[:, :, :], pb[:, :, :], bc8(rd[:, 2, :]), ALU.mult))
        prio = cst[0:S, C_PR:C_PR + 64].rearrange("p (b n) -> p b n", b=NB)
        for k, mk in enumerate((m1, m2)):
            seq(lambda e, k=k: e.tensor_reduce(rd[:, 3 + k, :], pb[:, :, :], axis=X, op=ALU.max))
            seq(lambda e, k=k: e.tensor_tensor(pc[:, :, :], pb[:, :, :], bc8(rd[:, 3 + k, :]), ALU.is_equal))
            seq(lambda e: e.tensor_tensor(pc[:, :, :], pc[:, :, :], prio, ALU.mult))
            seq(lambda e: e.tensor_reduce(rd[:, 5, :], pc[:, :, :], axis=X, op=ALU.max))
            seq(lambda e, mk=mk: e.tensor_tensor(mk[:, :, :], pc[:, :, :], bc8(rd[:, 5, :]), ALU.is_equal))
            if k == 0:
                seq(lambda e: e.scalar_tensor_tensor(pb[:, :, :], m1[:, :, :], -4.0, pb[:, :, :], ALU.mult, ALU.add))
        a = seq(lambda e: e.tensor_tensor(mb[:, :, :], m1[:, :, :], m2[:, :, :], ALU.add))
        mbf = mb[:, :, :].rearrange("p b n -> p (b n)")
        mm(ps[0:S, 0, 0:64], cst[0:S, C_LT:C_LT + S], mbf, True, True, a, bank_free[0])
        a = mm(ps[:, 1, 0:64], one64_128, mbf, True, True, a, bank_free[1], T["ones"], sig=True)
        seq(lambda e: e.tensor_tensor(rd[:, 5, :], rd[:, 3, :], rd[:, 4, :], ALU.add))
        seq(lambda e: e.reciprocal(rd[:, 6, :], rd[:, 5, :]))
        for k in range(2):
            T["rwt"] = seq(lambda e, k=k: e.tensor_tensor(rwt[:, k, :], rd[:, 3 + k, :], rd[:, 6, :], ALU.mult))
        seq(lambda e: e.tensor_copy(cn[:, :, :].rearrange("p b n -> p (b n)"), ps[:, 1, 0:64]), a)
        cne = cn[:, :, :].rearrange("p b n -> p n b")
        sc_f = sc[:, :, :].rearrange("p n b -> p (n b)")
        seq(lambda e: e.tensor_reduce(e8[:, 0, :], cne, axis=X, op=ALU.add))
        seq(lambda e: e.tensor_tensor(th[:, :, :], e8[:, 0, :].unsqueeze(2).to_broadcast([128, NE, 7]),
                                      cst[:, C_TH:C_TH + 7].unsqueeze(1).to_broadcast([128, NE, 7]), ALU.is_gt))
        seq(lambda e: e.tensor_reduce(e8[:, 1, :], th[:, :, :], axis=X, op=ALU.add))
        seq(lambda e: e.tensor_tensor_scan(e8[:, 2, :], one64[:, 0:NE], e8[:, 0, :], 0.0, ALU.mult, ALU.add), T["one64"])
        seq(lambda e: e.tensor_tensor_scan(e8[:, 3, :], one64[:, 0:NE], e8[:, 1, :], 0.0, ALU.mult, ALU.add))
        seq(lambda e: e.tensor_tensor(e8[:, 3, :], e8[:, 3, :], e8[:, 1, :], ALU.subtract))
        seq(lambda e: e.tensor_scalar(e8[:, 3, :], e8[:, 3, :], 128.0, None, ALU.mult))
        seq(lambda e: e.tensor_tensor(e8[:, 2, :], e8[:, 2, :], e8[:, 0, :], ALU.subtract))
        seq(lambda e: e.tensor_tensor(e8[:, 4, :], e8[:, 3, :], e8[:, 2, :], ALU.subtract))
        seq(lambda e: e.tensor_copy(sc[:, :, :], cne))
        stf = seg3[:, 0, :]
        seq(lambda e: e.tensor_tensor_scan(stf, one64[:, :], sc_f, 0.0, ALU.mult, ALU.add))
        seq(lambda e: e.tensor_tensor(sc_f, stf, sc_f, ALU.subtract))
        seq(lambda e: e.tensor_tensor(stt[:, :, :].rearrange("p b n -> p n b"), sc[:, :, :],
                                      e8[:, 4, :].unsqueeze(2).to_broadcast([128, NE, NB]), ALU.add))
        seq(lambda e: e.tensor_tensor(pc[:, :, :], stt[0:S, :, :],
                                      ps[0:S, 0, 0:64].rearrange("p (b n) -> p b n", b=NB), ALU.add))
        for k, mk in enumerate((m1, m2)):
            seq(lambda e, mk=mk: e.tensor_tensor(mk[:, :, :], mk[:, :, :], pc[:, :, :], ALU.mult))
            seq(lambda e, mk=mk, k=k: e.tensor_reduce(rd[:, k, :], mk[:, :, :], axis=X, op=ALU.add))
            T["idx"] = seq(lambda e, k=k: e.tensor_copy(idx[:, k, :], rd[:, k, :]))
        bank_free[0] = bank_free[1] = T["idx"]
        xsem = dsem("xsem")
        for b in range(NB):
            for k in range(2):
                T["xs_all"] = POOL.dma(lambda e, b=b, k=k: e.indirect_dma_start(
                    out=xs_d.ap(), out_offset=bass.IndirectOffsetOnAxis(ap=idx[:, k, b:b + 1], axis=0),
                    in_=y[:, b, :], in_offset=None), xsem, T["idx"], T["y", b], T["zero"])
        seq(lambda e: e.tensor_tensor(etf[:, :, :], cst[0:1, C_SL:C_SL + NT].unsqueeze(2).to_broadcast([1, NT, NE]),
                                      e8[0:1, 3, :].unsqueeze(1).to_broadcast([1, NT, NE]), ALU.is_ge))
        seq(lambda e: e.tensor_reduce(et1[:, :], etf[:, :, :], axis=X, op=ALU.add))
        T["eti"] = seq(lambda e: e.tensor_scalar(eti[:, :], et1[:, :], float(WC), -float(WC), ALU.mult, ALU.add))
        seq(lambda e: e.tensor_tensor(
            seg3[:, :, :], cst[:, C_SL:C_SL + NT].unsqueeze(2).to_broadcast([128, NT, 64]),
            stt[:, :, :].rearrange("p b n -> p (b n)").unsqueeze(1).to_broadcast([128, NT, 64]), ALU.is_ge))
        T["segc"] = seq(lambda e: e.tensor_reduce(segc[:, :], seg3[:, :, :], axis=X, op=ALU.add))
        rt.close()

        G = lambda name, shape, dt=f32: sbuf(root, name, shape, dt)
        RX, RV = 3, 4
        xs = G("xs", [128, RX, 256])
        xsT = G("xsT", [128, RX, 256])
        kq = G("kq", [128, 2, 512])
        sg = G("sg", [128, 2, 512])
        vv = G("vv", [128, RV, 256])
        u = G("u", [128, 2, 768])
        fm = G("fm", [128, 2, 256])
        ss = G("ss", [128, 2, 256])
        mc = G("mc", [128, RV, 128])
        tcm = G("tcm", [128, 2, 128])
        trm = G("trm", [128, 2, 128])
        pl = G("pl", [128, NT + 1])
        fl = G("fl", [128, 2, NT + 1])
        dc = G("dc", [128, 2, 512])
        ed = G("ed", [128, 2, 256])
        dr = G("dr", [128, 2, 256])
        si = G("si", [128, 2, 256])
        ktz = G("ktz", [128, 2, 4, 128])
        qT = G("qT", [128, 2, 2, 128])
        stz = G("stz", [128, 3, 4, 128])
        am = G("am", [128, 2, 4, 128])
        hz = G("hz", [128, 4, 2, 128])
        hv = G("hv", [128, 4, 2, 128])
        ok = G("ok", [128, 2, 256])
        o2 = G("o2", [128, 2, 256])
        sm4 = G("sm4", [128, 4, 8])
        qg = G("qg", [128, 2, 512])
        qgT = G("qgT", [128, 2, 512])
        tm = G("tm", [128, 2, 4, 128])
        oo = G("oo", [128, 2, 256])
        allt = [T["segc"], T["xs_all"]]
        done_att = (ACTE.sem, ACTE.n), (PE.sem, PE.n), (POOL.sem, POOL.n), (DVE.sem, DVE.n)
        T["z1"] = POOL.put(lambda e: e.memset(ktz[:, :, :, :], 0.0), *done_att, T["idx"])
        T["z2"] = POOL.put(lambda e: e.memset(stz[:, :, :, :], 0.0))
        T["z3"] = POOL.put(lambda e: e.memset(hz[:, 3, :, :], 0.0))
        T["z4"] = POOL.put(lambda e: e.memset(hv[:, 3, :, :], 0.0))
        T["z5"] = POOL.put(lambda e: e.memset(pl[:, 0:1], -1.0))
        T["hz", -1], T["hv", -1], T["pl", -1] = T["z3"], T["z4"], T["z5"]
        le, lc, gt = (cst[:, c:c + 128] for c in (C_LE, C_LC, C_GT))
        bd2 = cst[:, C_BD2:C_BD2 + 128].unsqueeze(1).to_broadcast([128, 2, 128])
        v4 = lambda a: a.rearrange("p (h n) -> p h n", h=4)
        v2 = lambda a: a.rearrange("p (h n) -> p h n", h=2)
        d_xs = [dsem(f"d_xs{i}") for i in range(RX)]

        def bankw(k):
            return bank_free.get(k)

        def g_load(t):
            T["xs", t] = SP.dma(lambda e: e.dma_start(xs[:, t % RX, :], xs_d[128 * t:128 * t + 128, :]), d_xs[t % RX],
                                T["xs_all"], W("xsT_p", t - RX), T["z1"])

        def g_x(t):
            for i in range(2):
                a = tr(ps[:, 4, 128 * i:128 * i + 128], xs[:, t % RX, 128 * i:128 * i + 128], 128, T["xs", t],
                       bankw(4), sig=i == 1)
            T["xsT_p", t] = a
            T["xsT", t] = bank_free[4] = ACTE.put(lambda e: e.activation(xsT[:, t % 2, :], ps[:, 4, 0:256], ACT.Copy),
                                                  a, W("proj", t - 2), T["z1"])
            if t + RX < NT:
                g_load(t + RX)

        def g_proj(t):
            def dyn(o, i, lo, n, start, stop):
                def f(e):
                    off = e.snap(regs[t], min_val=0, max_val=(NE - 1) * WC)
                    return e.matmul(o, xsT[:, t % 2, 128 * i:128 * i + 128],
                                    wm[:, bass.ds(off + (i * 768 + lo), n)], start=start, stop=stop)
                return f

            for i in range(2):
                PE.put(dyn(ps[:, t % 2, 0:256], i, 0, 256, i == 0, i == 1), bankw(t % 2), T["xsT", t],
                       *(T[f"wm{n}"] for n in range(NE)), sig=False)
            for i in range(2):
                a = mm(ps[:, t % 2, 256:512], xsT[:, t % 2, 128 * i:128 * i + 128], wqm[:, i, :], i == 0, i == 1,
                       T["wqm"], sig=i == 1)
            T["pkq", t] = a
            for i in range(2):
                a = PE.put(dyn(ps[:, 2, 0:512], i, 256, 512, i == 0, i == 1), bankw(2), sig=i == 1)
            T["proj", t] = a

        def g_softplus(t):
            r = t % 2
            ACTE.put(lambda e: e.activation(u[:, r, 0:512], ps[:, r, :], ACT.Abs), T["pkq", t], W("g8", t - 2),
                     T["z1"], T["g_all"])
            a = ACTE.put(lambda e: e.activation(u[:, r, 512:768], ps[:, 2, 256:512], ACT.Abs), T["proj", t])
            T["vv", t] = ACTE.put(lambda e: e.activation(vv[:, t % RV, :], ps[:, 2, 0:256], ACT.Copy),
                                  W("ov", t - RV), W("h_p", t - RV))
            a = ACTE.put(lambda e: e.activation(u[:, r, :], u[:, r, :], ACT.Exp, scale=-1.0), a)
            T["u", t] = ACTE.put(lambda e: e.activation(u[:, r, :], u[:, r, :], ACT.Ln, bias=1.0), a)

        def g_logsig(t):
            r = t % 2
            T["ls", t] = DVE.put(lambda e: e.scalar_tensor_tensor(sg[:, r, :], ps[:, r, :], 0.0, u[:, r, 0:512],
                                                                  ALU.min, ALU.subtract), T["u", t], W("kq", t - 2),
                                 T["z1"])
            T["g8", t] = bank_free[2] = DVE.put(lambda e: e.scalar_tensor_tensor(
                fm[:, r, :], ps[:, 2, 256:512], 0.0, u[:, r, 512:768], ALU.min, ALU.subtract), T["vv", t],
                W("G", t - 2), W("ss0", t - 2))

        def g_sig(t):
            r = t % 2
            T["sg", t] = ACTE.put(lambda e: e.activation(sg[:, r, :], sg[:, r, :], ACT.Exp), T["ls", t])
            c = T["ss0", t] = ACTE.put(lambda e: e.activation(ss[:, r, :], fm[:, r, :], ACT.Exp, scale=0.125),
                                       T["g8", t], W("si", t - 2), W("srem", t - 2))
            T["ss", t] = POOL.put(lambda e: e.tensor_scalar(ss[:, r, :], ss[:, r, :], -1.0, 1.0, ALU.mult, ALU.add), c)

        def g_kq(t):
            r = t % 2
            T["kq", t] = bank_free[r] = DVE.put(lambda e: e.tensor_tensor(kq[:, r, :], ps[:, r, :], sg[:, r, :],
                                                                         ALU.mult), T["sg", t],
                                                W("kqT_p", t - 2), W("h_p", t - 2))

        def g_mask(t):
            r = t % 2
            a = tr(ps[:, 7, 0:128], segc[:, t:t + 1].to_broadcast([128, 128]), 128, T["segc"], bankw(7), sig=True)
            row, col = ps[:, 7, 0:128], segc[:, t:t + 1]
            DVE.put(lambda e: e.scalar_tensor_tensor(mc[:, t % RV, :], row, col, le, ALU.is_equal, ALU.mult), a,
                    W("G", t - RV), W("am", t - RV), W("tm", t - RV), T["z1"])
            DVE.put(lambda e: e.scalar_tensor_tensor(tcm[:, r, :], row, col, lc, ALU.is_equal, ALU.mult), W("G", t - 2))
            T["msk", t] = DVE.put(lambda e: e.scalar_tensor_tensor(trm[:, r, :], row, col, gt, ALU.is_equal, ALU.mult))
            c = T["pl", t] = bank_free[7] = DVE.put(lambda e: e.tensor_copy(pl[:, t + 1:t + 2], ps[:, 7, 127:128]),
                                                    T["z5"])
            DVE.put(lambda e: e.tensor_tensor(fl[:, 0, t:t + 1], col, pl[:, t:t + 1], ALU.is_equal), T["pl", t - 1], c)
            T["fl", t] = DVE.put(lambda e: e.tensor_tensor(fl[:, 1, t:t + 1], col, pl[:, t + 1:t + 2], ALU.is_equal))

        def g_kqT(t):
            r = t % 2
            for i in range(4):
                a = tr(ps[:, 3, 128 * i:128 * i + 128], kq[:, r, 128 * i:128 * i + 128], 128, T["kq", t], bankw(3),
                       sig=i == 3)
            T["kqT_p", t] = a
            c = ACTE.put(lambda e: e.activation(qT[:, r, :, :].rearrange("p a n -> p (a n)"), ps[:, 3, 256:512],
                                                ACT.Copy), a, W("p2", t - 2), W("at", t - 2))
            for hb in range(2):
                c = ACTE.put(lambda e, hb=hb: e.activation(
                    ktz[64 * hb:64 * hb + 64, r, hb:4:2, :], v2(ps[64 * hb:64 * hb + 64, 3, 0:256]), ACT.Copy))
            T["kqT", t] = bank_free[3] = c

        def g_decay(t):
            r = t % 2
            mm(ps[:, 4, 0:256], tcm[:, r, :], fm[:, r, :], True, True, T["msk", t], T["g8", t], bankw(4))
            a = mm(ps[:, 4, 256:512], mc[:, t % RV, :], fm[:, r, :], True, True, sig=True)
            b = mm(ps[:, 5, 0:256], trm[:, r, :], fm[:, r, :], True, True, bankw(5), sig=True)
            T["G", t] = b
            c = T["ed", t] = ACTE.put(lambda e: e.activation(ed[:, r, :], ps[:, 4, 0:256], ACT.Exp, scale=-0.125), a,
                                      W("si", t - 2))
            T["dc", t] = bank_free[4] = ACTE.put(lambda e: e.activation(dc[:, r, :], ps[:, 4, :], ACT.Exp, scale=0.125),
                                                 W("o2", t - 2), W("qg", t - 2), W("qg0", t - 2))
            T["dr", t] = bank_free[5] = ACTE.put(lambda e: e.activation(dr[:, r, :], ps[:, 5, 0:256], ACT.Exp,
                                                                        scale=0.125), b, W("h_p", t - 2))

        def g_si(t):
            r = t % 2
            T["si", t] = POOL.put(lambda e: e.tensor_tensor(si[:, r, :], ss[:, r, :], ed[:, r, :], ALU.mult),
                                  T["ed", t], T["ss", t], W("p1", t - 2), W("siT_p", t - 2))
            T["srem", t] = DVE.put(lambda e: e.scalar_tensor_tensor(dr[:, r, :], dr[:, r, :], fl[:, 1, t:t + 1],
                                                                    ss[:, r, :], ALU.mult, ALU.mult), T["dr", t],
                                   T["fl", t], T["ss", t])

        def g_at(t):
            r = t % 2
            for h in range(4):
                a = mm(ps[:, 6, 128 * h:128 * h + 128], ktz[:, r, h, :], qT[:, r, h // 2, :], True, True,
                       T["kqT", t], bankw(6), sig=h == 3)
            T["at", t] = a
            T["am", t] = bank_free[6] = DVE.put(lambda e: e.tensor_tensor(
                am[:, r, :, :], v4(ps[:, 6, :]), mc[:, t % RV, :].unsqueeze(1).to_broadcast([128, 4, 128]), ALU.mult),
                a, T["msk", t], W("p1", t - 2))

        def g_state(t):
            r = t % 2
            for i in range(2):
                mm(ps[:, 5, 128 * i:128 * i + 128], kq[:, r, 128 * i:128 * i + 128], dr[:, r, 128 * i:128 * i + 128],
                   True, True, T["srem", t], T["kq", t], bankw(5))
                a = mm(ps[:, 5, 256 + 128 * i:384 + 128 * i], dr[:, r, 128 * i:128 * i + 128],
                       vv[:, t % RV, 128 * i:128 * i + 128], True, True, T["vv", t], sig=i == 1)
            T["h_p", t] = a
            T["hz", t] = DVE.put(lambda e: e.tensor_tensor(hz[:, t % 4, :, :], v2(ps[:, 5, 0:256]), bd2, ALU.mult), a,
                                 W("p2", t - 3), T["z3"])
            T["hv", t] = bank_free[5] = DVE.put(lambda e: e.tensor_tensor(hv[:, t % 4, :, :], v2(ps[:, 5, 256:512]),
                                                                          bd2, ALU.mult), a, W("ov", t - 3), T["z4"])

        def g_siT(t):
            for i in range(2):
                a = tr(ps[:, 3, 128 * i:128 * i + 128], si[:, t % 2, 128 * i:128 * i + 128], 128, T["si", t],
                       bankw(3), sig=i == 1)
            T["siT_p", t] = a
            for hb in range(2):
                c = ACTE.put(lambda e, hb=hb: e.activation(
                    stz[64 * hb:64 * hb + 64, t % 3, hb:4:2, :], v2(ps[64 * hb:64 * hb + 64, 3, 0:256]), ACT.Copy), a,
                    W("tm_p", t - 3), T["z2"])
            T["stz", t] = bank_free[3] = c

        def g_ok(t):
            r = t % 2
            for h in range(4):
                mm(ps[:, 7, 64 * h:64 * h + 64], am[:, r, h, :], si[:, r, 64 * h:64 * h + 64], True, True,
                   T["am", t], T["si", t], bankw(7))
            for i in range(2):
                a = mm(ps[:, 7, 256 + 128 * i:384 + 128 * i], qT[:, r, i, :], hz[:, (t - 1) % 4, i, :], True, True,
                       T["hz", t - 1], sig=i == 1)
            T["p1", t] = T["p2", t] = a
            d, d0 = dc[:, r, 0:256], dc[:, r, 256:512]
            first = fl[:, 0, t:t + 1]
            DVE.put(lambda e: e.tensor_tensor(ok[:, r, :], ps[:, 7, 0:256], d, ALU.mult), a, T["dc", t],
                    W("qg", t - 2), W("qg0", t - 2))
            T["o2", t] = bank_free[7] = DVE.put(lambda e: e.scalar_tensor_tensor(
                o2[:, r, :], ps[:, 7, 256:512], first, d0, ALU.mult, ALU.mult), T["fl", t])
            T["ok", t] = DVE.put(lambda e: e.tensor_tensor(ok[:, r, :], ok[:, r, :], o2[:, r, :], ALU.add),
                                 T["o2", t])

        def g_max(t):
            r = t % 2
            s4 = sm4[:, t % 4, :]
            b = DVE.put(lambda e: e.tensor_reduce(s4[:, 0:4], v4(ok[:, r, :]), axis=X, op=ALU.max), T["ok", t],
                        W("oo", t - 4))
            c = POOL.put(lambda e: e.tensor_tensor(v4(ok[:, r, :]), v4(ok[:, r, :]),
                                                   s4[:, 0:4].unsqueeze(2).to_broadcast([128, 4, 64]), ALU.subtract), b)
            T["eok", t] = ACTE.put(lambda e: e.activation(ok[:, r, :], ok[:, r, :], ACT.Exp), c)

        def g_qg(t):
            r = t % 2
            d, d0 = dc[:, r, 0:256], dc[:, r, 256:512]
            first = fl[:, 0, t:t + 1]
            s4 = sm4[:, t % 4, :]
            e0 = T["eok", t]
            T["qg", t] = POOL.put(lambda e: e.tensor_tensor(qg[:, r, 0:256], ok[:, r, :], d, ALU.mult), e0,
                                  W("qgT_p", t - 2))
            b = DVE.put(lambda e: e.tensor_reduce(s4[:, 4:8], v4(ok[:, r, :]), axis=X, op=ALU.add), e0)
            T["qg0", t] = DVE.put(lambda e: e.scalar_tensor_tensor(qg[:, r, 256:512], ok[:, r, :], first, d0,
                                                                   ALU.mult, ALU.mult), W("qgT_p", t - 2))
            T["rz", t] = DVE.put(lambda e: e.reciprocal(s4[:, 4:8], s4[:, 4:8]), b)

        def g_qgT(t):
            r = t % 2
            for i in range(4):
                a = tr(ps[:, 3, 128 * i:128 * i + 128], qg[:, r, 128 * i:128 * i + 128], 128, T["qg", t],
                       T["qg0", t], bankw(3), sig=i == 3)
            T["qgT_p", t] = a
            T["qgT", t] = bank_free[3] = ACTE.put(lambda e: e.activation(qgT[:, r, :], ps[:, 3, :], ACT.Copy), a,
                                                  W("ov", t - 2), W("tm_p", t - 2))

        def g_tm(t):
            r = t % 2
            for h in range(4):
                a = mm(ps[:, 6, 128 * h:128 * h + 128], stz[:, t % 3, h, :], qgT[:, r, 128 * (h // 2):128 * (h // 2) + 128],
                       True, True, T["stz", t], T["qgT", t], bankw(6), sig=h == 3)
            T["tm_p", t] = a
            T["tm", t] = bank_free[6] = DVE.put(lambda e: e.tensor_tensor(
                tm[:, r, :, :], v4(ps[:, 6, :]), mc[:, t % RV, :].unsqueeze(1).to_broadcast([128, 4, 128]), ALU.mult),
                a, W("ov", t - 2))

        osem = [dsem("osem0"), dsem("osem1")]

        def g_ov(t):
            r = t % 2
            for i in range(2):
                mm(ps[:, 7, 128 * i:128 * i + 128], qgT[:, r, 256 + 128 * i:384 + 128 * i], hv[:, (t - 1) % 4, i, :],
                   True, False, T["hv", t - 1], T["tm", t], bankw(7))
                for h in (2 * i, 2 * i + 1):
                    a = mm(ps[:, 7, 64 * h:64 * h + 64], tm[:, r, h, :], vv[:, t % RV, 64 * h:64 * h + 64], False,
                           h == 2 * i + 1, sig=h == 3)
            T["ov", t] = a
            c = DVE.put(lambda e: e.tensor_tensor(v4(oo[:, r, :]), v4(ps[:, 7, 0:256]),
                                                  sm4[:, t % 4, 4:8].unsqueeze(2).to_broadcast([128, 4, 64]), ALU.mult),
                        a, T["rz", t], W("od", t - 2))
            T["oo", t] = bank_free[7] = c
            T["od", t] = SP.dma(lambda e: e.dma_start(o_d[128 * t:128 * t + 128, :], oo[:, r, :]), osem[r], c)

        regs = []
        for t in range(RX):
            g_load(t)
        T["g_all"] = T["z5"]
        PE.put(lambda e: e.load(regs, eti[0:1, :]), T["eti"], sig=False)
        plan = [(g_ok, 2), (g_qgT, 3), (g_kq, 1), (g_proj, 0), (g_max, 2), (g_tm, 3), (g_kqT, 1), (g_decay, 1),
                (g_softplus, 0), (g_ov, 3), (g_si, 1), (g_at, 1), (g_mask, 0), (g_qg, 2), (g_x, -1), (g_siT, 1),
                (g_state, 1), (g_logsig, 0), (g_sig, 0)]
        for n in range(-1, NT + 3):
            for f, back in plan:
                if 0 <= n - back < NT:
                    f(n - back)

        fin = G("fin", [S, 4, 2, 256])
        fT = G("fT", [128, 2, 2, S])
        fr = G("fr", [S, NB, 4])
        gsem = [dsem(f"gsem{i}") for i in range(4)]
        d_out = dsem("d_out")
        fin_end = []

        def f_gather(b):
            for k in range(2):
                T["ga", b] = POOL.dma(lambda e, k=k: e.indirect_dma_start(
                    out=fin[:, b % 4, k, :], out_offset=None, in_=o_d.ap(),
                    in_offset=bass.IndirectOffsetOnAxis(ap=idx[:, k, b:b + 1], axis=0)), gsem[b % 4],
                    T["od", NT - 1], T["od", NT - 2], W("fs", b - 4))

        def f_sum(b):
            f0, f1 = fin[:, b % 4, 0, :], fin[:, b % 4, 1, :]
            a = DVE.put(lambda e: e.tensor_scalar(f0, f0, rwt[:, 0, b:b + 1], None, ALU.mult), T["ga", b])
            a = DVE.put(lambda e: e.scalar_tensor_tensor(f0, f1, rwt[:, 1, b:b + 1], f0, ALU.mult, ALU.add), a)
            a2 = ACTE.put(lambda e: e.activation(f1, f0, ACT.Square, accum_out=fr[:, b, 0:1]), a)
            a2 = POOL.put(lambda e: e.tensor_scalar(fr[:, b, 1:2], fr[:, b, 0:1], 1.0 / D, 1e-5, ALU.mult, ALU.add), a2)
            a2 = POOL.put(lambda e: e.tensor_tensor(fr[:, b, 2:3], fr[:, b, 1:2], epow[:, :], ALU.pow), a2)
            T["fs0", b] = (a, a2)

        def f_norm(b):
            f0 = fin[:, b % 4, 0, :]
            a = DVE.put(lambda e: e.scalar_tensor_tensor(f0, f0, fr[:, b, 2:3], rw_sb[:, 4, :], ALU.mult, ALU.mult),
                        *T["fs0", b])
            k0 = b % 2
            for i in range(2):
                a1 = tr(ps[:, k0, S * i:S * i + S], f0[:, 128 * i:128 * i + 128], S, a, bankw(k0), sig=i == 1)
            T["fs", b] = a1
            T["fT", b] = bank_free[k0] = ACTE.put(lambda e: e.activation(
                fT[:, b % 2, :, :].rearrange("p t n -> p (t n)"), ps[:, k0, 0:2 * S], ACT.Copy), a1, W("fo2", b - 2))

        def f_out(b):
            k0 = 2 + b % 2
            for i in range(2):
                a = mm(ps[0:S, k0, 0:256], fT[:, b % 2, i, :], wom[:, i, :], i == 0, i == 1, T["fT", b], T["wom"],
                       bankw(k0), sig=i == 1)
            T["fo2", b] = a
            c = bank_free[k0] = DVE.put(lambda e: e.tensor_tensor(x2[:, b, :], x2[:, b, :], ps[0:S, k0, 0:256],
                                                                  ALU.add), a)
            T["done"] = SP.dma(lambda e: e.dma_start(out[b], x2[:, b, :]), d_out, c)

        for n in range(NB + 3):
            for f, b in ((f_gather, n), (f_sum, n - 1), (f_norm, n - 2), (f_out, n - 3)):
                if 0 <= b < NB:
                    f(b)
        SP.put(lambda e: e.nop(), T["done"], T["zero"], T["xs_all"], T["od", NT - 1], T["od", NT - 2], sig=False)

        blk = root.enter_context(nc.Block())

        @blk.sync
        def _(e):
            SP.play(e)

        @blk.tensor
        def _(e):
            regs.extend(e.alloc_register(f"expert{t}") for t in range(NT))
            PE.play(e)

        @blk.vector
        def _(e):
            DVE.play(e)

        @blk.scalar
        def _(e):
            ACTE.play(e)

        @blk.gpsimd
        def _(e):
            POOL.play(e)


def constants():
    import numpy as np
    c = np.zeros((128, C_N), np.float32)
    j, i = np.arange(128)[:, None], np.arange(128)[None, :]
    c[:, C_ID:C_ID + 128] = j == i
    c[:, C_LE:C_LE + 128] = j <= i
    c[:, C_LC:C_LC + 128] = (j <= i) * 1.0 - (j <= 63) * 1.0
    c[:, C_GT:C_GT + 128] = j > i
    c[:, C_LT:C_LT + 128] = j < i
    c[:, C_BD:C_BD + 128] = j // 16 == i // 16
    c[:, C_BD2:C_BD2 + 128] = j // 64 == i // 64
    c[:, C_HM:C_HM + 8] = j // 16 == np.arange(8)[None, :]
    c[:, C_PR:C_PR + 64] = 8 - np.arange(64)[None, :] % 8
    c[:, C_SL:C_SL + 21] = 128 * np.arange(21)[None, :] + j
    c[:, C_TH:C_TH + 7] = 128 * np.arange(7)[None, :]
    c[:, C_CB:C_CB + 112] = np.where(i[:, 0:112] > j, -1e30, 0.0)
    return c


def kernel(**inputs):
    import numpy as np
    import concourse.bacc as bacc
    from concourse.bass_utils import run_bass_kernel_spmd

    g = {k: np.asarray(v) for k, v in inputs.items()}
    c = np.ascontiguousarray
    ffn = np.concatenate([g["L0_ffn_Wk"].transpose(0, 2, 1), g["L0_ffn_Wv"].transpose(0, 2, 1),
                          g["L0_ffn_Wf"].transpose(0, 2, 1)], axis=2)

    def head_rows(w):
        r = np.zeros((4, 4, 32, 256), w.dtype)
        r[:, :, 0:16, :] = w.reshape(4, 4, 16, 256)
        return r.reshape(4, 128, 256)

    wxv = np.zeros((128, 128), g["L0_xattn_Wv"].dtype)
    for j in range(0, 128, 32):
        wxv[j:j + 16, j:j + 16] = g["L0_xattn_Wv"]
    arrays = {
        "x": g["x"], "ctx": g["ctx_1024"], "ctxT": g["ctx_1024"].transpose(0, 2, 1), "mask": g["mask_Bx1xSxS2_ik1"],
        "wself": np.stack([g["L0_attn_Wq"], g["L0_attn_Wk"], g["L0_attn_Wv"]]),
        "wos": head_rows(g["L0_attn_Wo"]),
        "bself": np.stack([g["L0_attn_bq"][0:128], g["L0_attn_bq"][128:], g["L0_attn_bk"][0:128],
                           g["L0_attn_bk"][128:]], axis=1),
        "wxq": np.tile(g["L0_xattn_Wq"], (1, 8)), "wxk": np.tile(g["L0_xattn_Wk"], (1, 8)),
        "wxv": wxv, "wxo": head_rows(g["L0_xattn_Wo"].T),
        "rows": np.concatenate([g["L0_attn_bv"], g["L0_attn_bo"], g["L0_xattn_bo"], g["L0_ffn_norm_w"],
                                g["L0_ffn_gnorm_w"]]),
        "wg": g["L0_ffn_Wg"].T, "wmoe": ffn, "wq_moe": g["L0_ffn_Wq"].T, "wo_moe": g["L0_ffn_Wo"].T,
        "consts": constants(),
    }
    arrays = {"in_" + k: c(v) for k, v in arrays.items()}
    nc = bacc.Bacc("TRN2", target_bir_lowering=False, num_devices=1)
    args = [nc.dram_tensor(k, a.shape, mybir.dt.from_np(a.dtype), kind="ExternalInput").ap() for k, a in arrays.items()]
    args.append(nc.dram_tensor("out0", (NB, S, D), mybir.dt.float32, kind="ExternalOutput").ap())
    decoder_kernel(nc, *args)
    r = run_bass_kernel_spmd(nc, [arrays], core_ids=[0])
    return r.results[0]["out0"]
```
